# Optimizing a Trainium2 kernel written in Bass

```python
import numpy as np
import jax
import jax.numpy as jnp

def _softmax(x, axis=-1):
    return jax.nn.softmax(x, axis=axis)

def _gelu(x):
    return jax.nn.gelu(x, approximate=True)

def _silu(x):
    return jax.nn.silu(x)

def _sigmoid(x):
    return jax.nn.sigmoid(x)

def _layernorm(x, axis=-1, eps=1e-05):
    m = jnp.mean(x, axis=axis, keepdims=True)
    v = jnp.var(x, axis=axis, keepdims=True)
    return (x - m) / jnp.sqrt(v + eps)

def _scatter_add(tgt, idx, src, axis=0):
    return tgt.at[idx].add(src)

def _segment_sum(src, seg, n):
    return jax.ops.segment_sum(src, seg, n)
kernel_name = 'mk_flamingo_gated_d2_seqx_r4_08249f'

def setup_inputs(seed: int=0):
    np.random.seed(seed)
    _w = jnp.asarray

    def _rec_inputs():
        import jax
        import jax.numpy as jnp
        _rk = jax.random.key(seed)
        x = -0.0003929 + 0.9999 * jax.random.normal(jax.random.fold_in(_rk, 1), (16, 112, 256), jnp.float32)
        _lenS = 112 - jax.random.randint(jax.random.fold_in(_rk, 7), (16,), 0, max(1, 112 // 4) + 1, jnp.int32)
        _lenS2 = 375 - jax.random.randint(jax.random.fold_in(_rk, 8), (16,), 0, max(1, 375 // 4) + 1, jnp.int32)
        _ctx_768P = jax.random.normal(jax.random.fold_in(_rk, 11), (16, 16, 192), jnp.float32)
        _ctx_768c = jax.random.dirichlet(jax.random.fold_in(_rk, 511), 0.3 * jnp.ones((16,), jnp.float32), (16, 375))
        _ctx_768t = jnp.einsum('bsk,bkd->bsd', _ctx_768c, _ctx_768P)
        _ctx_768t = _ctx_768t * jax.lax.rsqrt(jnp.mean(jnp.square(_ctx_768t)) + 1e-12) * 0.953939
        ctx_768 = 2.09791e-05 + 1.00001 * (_ctx_768t + 0.3 * jax.random.normal(jax.random.fold_in(_rk, 611), (16, 375, 192), jnp.float32))
        _g = jax.random.normal(jax.random.fold_in(_rk, 9001), (2, 2), jnp.float32)
        _g = jnp.sign(_g) * jnp.maximum(jnp.abs(_g), 1.0) + (_g == 0) * 1.0
        g_xattn = _g[0]
        g_ffn = _g[1]
        return (x, ctx_768, g_xattn, g_ffn)
    x, ctx_768, g_xattn, g_ffn = _rec_inputs()

    def _L0_xattn_setup():
        import jax, jax.numpy as jnp
        import numpy as np
        QUERY_DIM = 256
        KEY_DIM = 192
        NUM_HEADS = 16
        HEAD_DIM = QUERY_DIM // NUM_HEADS
        SCALE = HEAD_DIM ** (-0.5)
        key = jax.random.key(seed)
        ks = jax.random.split(key, 11)
        B, Nq, Nk = (4, 1024, 256)
        s_q = QUERY_DIM ** (-0.5)
        s_k = KEY_DIM ** (-0.5)
        return {'query': jax.random.normal(ks[0], (B, Nq, QUERY_DIM), jnp.float32), 'key': jax.random.normal(ks[1], (B, Nk, KEY_DIM), jnp.float32), 'value': jax.random.normal(ks[2], (B, Nk, KEY_DIM), jnp.float32), 'Wq': jax.random.normal(ks[3], (QUERY_DIM, QUERY_DIM), jnp.float32) * s_q, 'bq': jnp.zeros((QUERY_DIM,), jnp.float32), 'Wk': jax.random.normal(ks[4], (KEY_DIM, QUERY_DIM), jnp.float32) * s_k, 'bk': jnp.zeros((QUERY_DIM,), jnp.float32), 'Wv': jax.random.normal(ks[5], (KEY_DIM, QUERY_DIM), jnp.float32) * s_k, 'bv': jnp.zeros((QUERY_DIM,), jnp.float32), 'Wo': jax.random.normal(ks[6], (QUERY_DIM, QUERY_DIM), jnp.float32) * s_q, 'bo': jnp.zeros((QUERY_DIM,), jnp.float32)}
    _L0_xattn_all = _L0_xattn_setup()
    _L0_xattn_in = {k: v for k, v in _L0_xattn_all.items() if k in ('Wq', 'bq', 'Wk', 'bk', 'Wv', 'bv', 'Wo', 'bo')}
    del _L0_xattn_all

    def _L0_ffn_setup():
        import jax, jax.numpy as jnp
        import numpy as np
        EXPERTS = 8
        TOP_K = 2

        def swiglu(x, w1, w2, w3):
            h = x @ w1
            return h * jax.nn.sigmoid(h) * (x @ w2) @ w3
        key = jax.random.key(seed)
        ks = jax.random.split(key, 9)
        B, S, D = (4, 512, 256)
        H = 2 * D
        s = 0.02
        x = jax.random.normal(ks[0], (B, S, D), dtype=jnp.float32)
        gate_w = jax.random.normal(ks[1], (D, EXPERTS), dtype=jnp.float32) * s
        ew1 = jax.random.normal(ks[2], (EXPERTS, D, H), dtype=jnp.float32) * s
        ew2 = jax.random.normal(ks[3], (EXPERTS, D, H), dtype=jnp.float32) * s
        ew3 = jax.random.normal(ks[4], (EXPERTS, H, D), dtype=jnp.float32) * s
        sw1 = jax.random.normal(ks[5], (D, H), dtype=jnp.float32) * s
        sw2 = jax.random.normal(ks[6], (D, H), dtype=jnp.float32) * s
        sw3 = jax.random.normal(ks[7], (H, D), dtype=jnp.float32) * s
        return {'x': x, 'gate_w': gate_w, 'ew1': ew1, 'ew2': ew2, 'ew3': ew3, 'sw1': sw1, 'sw2': sw2, 'sw3': sw3}
    _L0_ffn_all = _L0_ffn_setup()
    _L0_ffn_in = {k: v for k, v in _L0_ffn_all.items() if k in ('gate_w', 'ew1', 'ew2', 'ew3', 'sw1', 'sw2', 'sw3')}
    del _L0_ffn_all

    def _L1_xattn_setup():
        import jax, jax.numpy as jnp
        import numpy as np
        HEADS = 16
        DIM_HEAD = 64
        QUERY_DIM = 256
        CONTEXT_DIM = 192
        INNER = HEADS * DIM_HEAD
        SCALE = DIM_HEAD ** (-0.5)
        key = jax.random.key(seed)
        ks = jax.random.split(key, 7)
        B, Sq, Skv = (4, 512, 512)
        x = jax.random.normal(ks[0], (B, Sq, QUERY_DIM), dtype=jnp.float32)
        context = jax.random.normal(ks[1], (B, Skv, CONTEXT_DIM), dtype=jnp.float32)
        w_q = jax.random.normal(ks[2], (QUERY_DIM, INNER), dtype=jnp.float32) / np.sqrt(QUERY_DIM)
        w_k = jax.random.normal(ks[3], (CONTEXT_DIM, INNER), dtype=jnp.float32) / np.sqrt(CONTEXT_DIM)
        w_v = jax.random.normal(ks[4], (CONTEXT_DIM, INNER), dtype=jnp.float32) / np.sqrt(CONTEXT_DIM)
        w_o = jax.random.normal(ks[5], (INNER, QUERY_DIM), dtype=jnp.float32) / np.sqrt(INNER)
        b_o = jax.random.normal(ks[6], (QUERY_DIM,), dtype=jnp.float32) * 0.02
        return {'x': x, 'context': context, 'w_q': w_q, 'w_k': w_k, 'w_v': w_v, 'w_o': w_o, 'b_o': b_o}
    _L1_xattn_all = _L1_xattn_setup()
    _L1_xattn_in = {k: v for k, v in _L1_xattn_all.items() if k in ('w_q', 'w_k', 'w_v', 'w_o', 'b_o')}
    del _L1_xattn_all

    def _L1_ffn_setup():
        import jax, jax.numpy as jnp
        import numpy as np
        import math
        B, S, H, I, E = (4, 512, 256, 1024, 8)
        TOP_K = 2
        CAPACITY_FACTOR = 1.25
        key = jax.random.key(seed)
        k1, k2, k3, k4, k5 = jax.random.split(key, 5)
        x = jax.random.normal(k1, (B, S, H), dtype=jnp.float32)
        W_router = jax.random.normal(k2, (E, H), dtype=jnp.float32) * (1.0 / math.sqrt(H))
        b_router = jnp.zeros((E,), dtype=jnp.float32)
        experts_inter = jax.random.normal(k3, (E, H, I), dtype=jnp.float32) * 0.02
        experts_out = jax.random.normal(k4, (E, I, H), dtype=jnp.float32) * 0.02
        return {'x': x, 'W_router': W_router, 'b_router': b_router, 'experts_inter': experts_inter, 'experts_out': experts_out}
    _L1_ffn_all = _L1_ffn_setup()
    _L1_ffn_in = {k: v for k, v in _L1_ffn_all.items() if k in ('W_router', 'b_router', 'experts_inter', 'experts_out')}
    del _L1_ffn_all
    return {'x': x, 'ctx_768': ctx_768, 'g_xattn': g_xattn, 'g_ffn': g_ffn, 'L0_xattn_Wq': _L0_xattn_in['Wq'], 'L0_xattn_bq': _L0_xattn_in['bq'], 'L0_xattn_Wk': _L0_xattn_in['Wk'], 'L0_xattn_bk': _L0_xattn_in['bk'], 'L0_xattn_Wv': _L0_xattn_in['Wv'], 'L0_xattn_bv': _L0_xattn_in['bv'], 'L0_xattn_Wo': _L0_xattn_in['Wo'], 'L0_xattn_bo': _L0_xattn_in['bo'], 'L0_ffn_gate_w': _L0_ffn_in['gate_w'], 'L0_ffn_ew1': _L0_ffn_in['ew1'], 'L0_ffn_ew2': _L0_ffn_in['ew2'], 'L0_ffn_ew3': _L0_ffn_in['ew3'], 'L0_ffn_sw1': _L0_ffn_in['sw1'], 'L0_ffn_sw2': _L0_ffn_in['sw2'], 'L0_ffn_sw3': _L0_ffn_in['sw3'], 'L1_xattn_w_q': _L1_xattn_in['w_q'], 'L1_xattn_w_k': _L1_xattn_in['w_k'], 'L1_xattn_w_v': _L1_xattn_in['w_v'], 'L1_xattn_w_o': _L1_xattn_in['w_o'], 'L1_xattn_b_o': _L1_xattn_in['b_o'], 'L1_ffn_W_router': _L1_ffn_in['W_router'], 'L1_ffn_b_router': _L1_ffn_in['b_router'], 'L1_ffn_experts_inter': _L1_ffn_in['experts_inter'], 'L1_ffn_experts_out': _L1_ffn_in['experts_out']}

def reference(x, ctx_768, g_xattn, g_ffn, L0_xattn_Wq, L0_xattn_bq, L0_xattn_Wk, L0_xattn_bk, L0_xattn_Wv, L0_xattn_bv, L0_xattn_Wo, L0_xattn_bo, L0_ffn_gate_w, L0_ffn_ew1, L0_ffn_ew2, L0_ffn_ew3, L0_ffn_sw1, L0_ffn_sw2, L0_ffn_sw3, L1_xattn_w_q, L1_xattn_w_k, L1_xattn_w_v, L1_xattn_w_o, L1_xattn_b_o, L1_ffn_W_router, L1_ffn_b_router, L1_ffn_experts_inter, L1_ffn_experts_out):
    import jax
    import jax.numpy as jnp

    def _L0_xattn_ref(query, key, value, Wq, bq, Wk, bk, Wv, bv, Wo, bo):
        import jax, jax.numpy as jnp
        import numpy as np
        QUERY_DIM = 256
        KEY_DIM = 192
        NUM_HEADS = 16
        HEAD_DIM = QUERY_DIM // NUM_HEADS
        SCALE = HEAD_DIM ** (-0.5)
        B, Nq, _ = query.shape
        Nk = key.shape[1]
        q = (query @ Wq + bq).reshape(B, Nq, NUM_HEADS, HEAD_DIM).transpose(0, 2, 1, 3)
        k = (key @ Wk + bk).reshape(B, Nk, NUM_HEADS, HEAD_DIM).transpose(0, 2, 1, 3)
        v = (value @ Wv + bv).reshape(B, Nk, NUM_HEADS, HEAD_DIM).transpose(0, 2, 1, 3)
        attn = jnp.einsum('bhqd,bhkd->bhqk', q, k) * SCALE
        attn = jax.nn.softmax(attn, axis=-1)
        out = jnp.einsum('bhqk,bhkd->bhqd', attn, v)
        out = out.transpose(0, 2, 1, 3).reshape(B, Nq, QUERY_DIM)
        return out @ Wo + bo

    def _L0_ffn_ref(x, gate_w, ew1, ew2, ew3, sw1, sw2, sw3):
        import jax, jax.numpy as jnp
        import numpy as np
        EXPERTS = 8
        TOP_K = 2

        def swiglu(x, w1, w2, w3):
            h = x @ w1
            return h * jax.nn.sigmoid(h) * (x @ w2) @ w3
        B, S, D = x.shape
        gate_out = x @ gate_w
        top_v, top_i = jax.lax.top_k(gate_out, TOP_K)
        masked = jnp.full_like(gate_out, -1e+20)
        bi = jnp.arange(B)[:, None, None]
        si = jnp.arange(S)[None, :, None]
        masked = masked.at[bi, si, top_i].set(top_v)
        probs = jax.nn.softmax(masked, axis=-1)
        chosen = jnp.zeros_like(gate_out, dtype=bool).at[bi, si, top_i].set(True)
        w = jnp.where(chosen, probs, 0.0)

        def one_expert(w1, w2, w3, we):
            return swiglu(x, w1, w2, w3) * we[..., None]
        out = jax.vmap(one_expert, in_axes=(0, 0, 0, 2))(ew1, ew2, ew3, w).sum(0)
        out = out + swiglu(x, sw1, sw2, sw3)
        return out

    def _L1_xattn_ref(x, context, w_q, w_k, w_v, w_o, b_o):
        import jax, jax.numpy as jnp
        import numpy as np
        HEADS = 16
        DIM_HEAD = 64
        QUERY_DIM = 256
        CONTEXT_DIM = 192
        INNER = HEADS * DIM_HEAD
        SCALE = DIM_HEAD ** (-0.5)
        B, Sq, _ = x.shape
        Skv = context.shape[1]
        q = (x @ w_q).reshape(B, Sq, HEADS, DIM_HEAD).transpose(0, 2, 1, 3)
        k = (context @ w_k).reshape(B, Skv, HEADS, DIM_HEAD).transpose(0, 2, 1, 3)
        v = (context @ w_v).reshape(B, Skv, HEADS, DIM_HEAD).transpose(0, 2, 1, 3)
        sim = jnp.einsum('bhid,bhjd->bhij', q, k) * SCALE
        attn = jax.nn.softmax(sim, axis=-1)
        out = jnp.einsum('bhij,bhjd->bhid', attn, v)
        out = out.transpose(0, 2, 1, 3).reshape(B, Sq, INNER)
        return out @ w_o + b_o

    def _L1_ffn_ref(x, W_router, b_router, experts_inter, experts_out):
        import jax, jax.numpy as jnp
        import numpy as np
        import math
        B, S, H, I, E = (4, 512, 256, 1024, 8)
        TOP_K = 2
        CAPACITY_FACTOR = 1.25
        b, s, h = x.shape
        e = experts_inter.shape[0]
        T = b * s
        capacity = math.ceil(T / e * CAPACITY_FACTOR)
        x_flat = x.reshape(T, h)
        logits = x_flat @ W_router.T + b_router
        weights_flat = jax.nn.softmax(logits, axis=-1)
        top_vals, top_idx = jax.lax.top_k(weights_flat, TOP_K)
        topk_flat = jnp.zeros_like(weights_flat).at[jnp.arange(T)[:, None], top_idx].set(top_vals)
        routing_mask = (topk_flat > 0).astype(jnp.int32)
        order = jnp.argsort(-routing_mask, axis=0, stable=True)
        sorted_mask = jnp.take_along_axis(routing_mask, order, axis=0)
        sorted_mask = sorted_mask[:capacity]
        sorted_idx = order[:capacity]
        used_tokens = (sorted_idx * sorted_mask).reshape(-1)
        mask_flat = sorted_mask.reshape(-1).astype(x.dtype)
        inputs_tokens = x_flat[used_tokens] * mask_flat[:, None]
        inputs_tokens = inputs_tokens.reshape(capacity, e, h)
        inputs_weights = jnp.take_along_axis(topk_flat, sorted_idx, axis=0)
        hmid = jnp.einsum('ceh,ehi->cei', inputs_tokens, experts_inter)
        hmid = jax.nn.relu(hmid)
        out = jnp.einsum('cei,eih->ceh', hmid, experts_out)
        out = out * inputs_weights[:, :, None]
        combined = jnp.zeros((T, h), dtype=x.dtype).at[used_tokens].add(out.reshape(-1, h))
        return combined.reshape(b, s, h)
    x = x + jnp.tanh(g_xattn[0]) * _L0_xattn_ref(_layernorm(x, axis=-1), ctx_768, ctx_768, L0_xattn_Wq, L0_xattn_bq, L0_xattn_Wk, L0_xattn_bk, L0_xattn_Wv, L0_xattn_bv, L0_xattn_Wo, L0_xattn_bo)
    x = x + jnp.tanh(g_ffn[0]) * _L0_ffn_ref(_layernorm(x, axis=-1), L0_ffn_gate_w, L0_ffn_ew1, L0_ffn_ew2, L0_ffn_ew3, L0_ffn_sw1, L0_ffn_sw2, L0_ffn_sw3)
    x = x + jnp.tanh(g_xattn[1]) * _L1_xattn_ref(_layernorm(x, axis=-1), ctx_768, L1_xattn_w_q, L1_xattn_w_k, L1_xattn_w_v, L1_xattn_w_o, L1_xattn_b_o)
    x = x + jnp.tanh(g_ffn[1]) * _L1_ffn_ref(_layernorm(x, axis=-1), L1_ffn_W_router, L1_ffn_b_router, L1_ffn_experts_inter, L1_ffn_experts_out)
    return x

_drawn_inputs = setup_inputs


def setup_inputs(seed=0):
    import zlib

    import numpy as np

    out = dict(_drawn_inputs(seed))
    spreads = {'g_ffn': (-1.0, 0.6),
     'L0_xattn_bq': (0.0, 0.516),
     'L0_xattn_bk': (0.0, 2.0),
     'L0_xattn_bv': (0.0, 0.1),
     'L0_xattn_bo': (0.0, 0.1),
     'L1_ffn_b_router': (0.0, 2.0)}
    factors = {'L0_ffn_gate_w': 5.71,
     'L0_ffn_ew1': 5.083,
     'L0_ffn_ew2': 5.004,
     'L0_ffn_ew3': 5.023,
     'L0_ffn_sw1': 3.632,
     'L0_ffn_sw2': 3.55,
     'L0_ffn_sw3': 3.607,
     'L1_xattn_b_o': 3.339,
     'L1_ffn_W_router': 4.245,
     'L1_ffn_experts_inter': 4.22,
     'L1_ffn_experts_out': 3.497}
    for name, (base, spread) in spreads.items():
        noise = np.random.default_rng([zlib.crc32(name.encode()), seed]).standard_normal(out[name].shape)
        drawn = base * np.exp(spread * noise) if base else spread * noise
        out[name] = jnp.asarray(drawn.astype(out[name].dtype))
    for name, factor in factors.items():
        out[name] = (out[name] * factor).astype(out[name].dtype)
    return out
```

```python
from contextlib import ExitStack

import concourse.bass as bass
from concourse import mybir

F32 = mybir.dt.float32
F32R = mybir.dt.float32r
I32 = mybir.dt.int32
BF16 = mybir.dt.bfloat16
ALU = mybir.AluOpType
ACT = mybir.ActivationFunctionType
AX = mybir.AxisListType

NB = 16
NQ = 112
D = 256
CD = 192
NK = 375
NKP = NK + 1
KC = 125
NC = NK // KC
H = 16
EPS = 1e-5
S_AHEAD, MAX_AHEAD, EXP_AHEAD = 3, 3, 2
S_BANK = (0, 1, 2) * 4 + (0, 1, 0, 2)
S_BACK = [next(n for n in range(1, H + 1) if S_BANK[(h - n) % H] == S_BANK[h]) for h in range(H)]
T_BANKS = 2
P_RING = 4
PT_RING = 8
O_BLOCKS = 4


class AttnShape:

    def __init__(self, tag, dh, bias):
        self.tag, self.dh, self.bias = tag, dh, bias
        self.inner = H * dh
        self.mt = self.inner // 128
        self.hpt = H // self.mt
        self.scale = float(dh) ** -0.5
        self.variants = self.hpt if dh == 16 else 1
        self.group = 4 if dh == 16 else 2
        self.vw = 128 // self.group
        self.ngroups = H // self.group
        self.turn = 5
        self.late_norm = dh == 16
        self.project_at = 3
        self.nout = self.ngroups // O_BLOCKS
        self.mq = self.mt // 2
        self.vparts = 1 if dh == 16 else 2
        self.vwide = self.inner // self.vparts
        self.vheads = H // self.vparts
        self.p_banks = 1 if dh == 16 else 2
        v = [[("v", part, c) for c in range(NC)] for part in range(self.vparts)]
        if dh == 16:
            at = {6: [("x", 0)], 7: [("x", 1)], 8: [("q", 0)], 10: [("k", 0)], 12: [("k", 1)], 15: [("q", 1)],
                  17: [v[0][0]], 19: [v[0][1]], 20: [v[0][2]]}
            self.split_at = 5
        else:
            at = {6: [("x", 0)], 7: [("x", 1)], 8: [("n", 0)], 9: [("q", 0), ("k", 0)], 10: [("n", 1), ("k", 1)], 11: [v[0][0]], 12: [("k", 2)], 13: [("q", 1)], 14: [v[0][1]], 15: [("k", 3)], 16: [v[0][2], ("k", 4)], 17: [("k", 5)], 18: [v[1][0]], 19: [v[1][1], ("k", 6)], 20: [("k", 7)], 21: [v[1][2]]}
            self.split_at = 6
        self.next_at, self.this_at = self.split_steps(at)
        self.next_out, self.this_out = self.split_steps({s + 1: ps for s, ps in at.items()})
        self.order = [p for s in sorted(at) for p in at[s]]
        self.before = [p for s in sorted(self.next_at) for p in self.next_at[s]]
        self.before_out = [p for s in sorted(self.next_out) for p in self.next_out[s]]
        self.behind_y = next(p for s in sorted(at) if s > H + self.project_at for p in at[s])
        self.np = len(self.order)
        assert self.np % self.p_banks == 0
        self.scalar_only = "n" if dh == 16 else "nv"
        self.early = [p for p in self.order if p[0] in self.scalar_only or p[0] != "v"]
        self.late = [p for p in self.order if p[0] not in self.scalar_only]
        self.last_v = [("v", part, NC - 1) for part in range(self.vparts)]

    @staticmethod
    def split_steps(at):
        assert max(at) - H < min(at)
        return {s: ps for s, ps in at.items() if s < H}, {s - H: ps for s, ps in at.items() if s >= H}

    def piece(self, p):
        return self.order.index(p)

    def scores_need(self, h):
        return max(("k", h // self.hpt), ("q", h // (H // 2)), key=self.piece)

    def high(self, t, p):
        return t * len(self.early) + self.early.index(p) + 1

    def out(self, t, p):
        return t * len(self.late) + self.late.index(p) + 1

    def pv_step(self, g):
        return self.group * g + self.group + 1


def walk(eng, turn, step):
    for h in range(turn):
        step(0, h, False, True)
    with eng.Fori(0, NB - 1) as i:
        for h in range(turn, H):
            step(i, h, True, True)
        for h in range(turn):
            step(i + 1, h, True, True)
    for h in range(turn, H):
        step(NB - 1, h, True, False)


def wait(eng, sem, value):
    if not (isinstance(value, int) and value <= 0):
        eng.wait_ge(sem, value)


def attention(nc, keep, A, x_sb, ident, tg, tg_col, raw, raw_loaded, dram, load_experts=None):
    T = A.tag
    ctx = ExitStack()

    def sb(name, shape, dt=F32):
        return ctx.enter_context(nc.sbuf_tensor(f"{T}_{name}", shape, dt))

    def sem(name):
        return keep.enter_context(nc.semaphore(f"{T}_{name}"))

    wq_h, wq_l = sb("wq_h", [128, 2, A.inner], F32R), sb("wq_l", [128, 2, A.inner], F32R)
    wk_h, wk_l = sb("wk_h", [128, 2, A.inner], F32R), sb("wk_l", [128, 2, A.inner], F32R)
    wv_h, wv_l = sb("wv_h", [128, 2, A.inner], F32R), sb("wv_l", [128, 2, A.inner], F32R)
    wo = sb("wo", [128, A.ngroups, D])
    bo = sb("bo", [128, D])
    if A.bias:
        kT_h, kT_l = sb("kT_h", [128, A.mt, NKP], F32R), sb("kT_l", [128, A.mt, NKP], F32R)
        qT_h = sb("qT_h", [128, A.mt, A.variants, NQ], F32R)
    else:
        k_both = sb("k_both", [128, A.mt, 2, NKP], F32R)
        q_twice = sb("q_twice", [128, A.mt, 2, NQ], F32R)
        q_rows = sb("q_rows", [128, A.inner])
    qT_l = sb("qT_l", [128, A.mt, A.variants, NQ], F32R)
    v_sb = sb("v_sb", [128, NC, H, A.vw])
    ctx_raw = sb("ctx_raw", [128, 2, NKP])
    ctx_h, ctx_l = sb("ctx_h", [128, NKP], F32R), sb("ctx_l", [128, NKP], F32R)
    ctx_b = sb("ctx_b", [128, NKP], F32R)
    xn = sb("xn", [128, D])
    xT_h, xT_l = sb("xT_h", [128, 2, NQ], F32R), sb("xT_l", [128, 2, NQ], F32R)
    probs, pT = sb("probs", [128, P_RING, NKP]), sb("pT", [128, PT_RING, NC * NQ])
    oT = sb("oT", [128, A.ngroups, NQ])
    if not A.bias:
        y_sb = sb("y_sb", [128, D])
    nmax, rsum, rinv = sb("nmax", [128, H]), sb("rsum", [128, H]), sb("rinv", [128, H])
    stats, mv = sb("stats", [128, NB, 6]), sb("mv", [128, NB, 2])
    var, rstd, tmp = sb("var", [128, NB]), sb("rstd", [128, NB]), sb("tmp", [128, NB])
    if A.bias:
        bq, bk, bv = sb("bq", [128, A.mt]), sb("bk", [128, A.mt]), sb("bv", [128, A.inner])
        head_mask = sb("head_mask", [128, A.hpt, 1])
        q_h = sb("q_h", [128, NQ], F32R)
        q_l = sb("q_l", [128, NQ], F32R)
        spare = raw.rearrange("p k c n -> p k (c n)")
        inv_wide = spare[:, 0, 0:H * A.vw].rearrange("p (h w) -> p h w", h=H)
        o_inv = spare[:, 1, 0:O_BLOCKS * NQ]
        q_t = spare[:, 2, 0:NQ]
        y_sb = spare[:, 2, D:2 * D]

    def pb(name):
        return ctx.enter_context(nc.psum_tensor(f"{T}_{name}", [128, 512], F32))

    s_ps = [pb(f"s_ps{n}") for n in range(max(S_BANK) + 1)]
    t_ps = [pb(f"t_ps{n}") for n in range(T_BANKS)]
    o_ps = pb("o_ps")
    p_ps = [pb(f"p_ps{n}") for n in range(A.p_banks)]
    y_ps = pb("y_ps") if A.bias else p_ps[A.piece(A.behind_y) % A.p_banks]

    small_loaded = sem("small_loaded")
    ctx_loaded = sem("ctx_loaded")
    w_high = sem("w_high")
    w_split = sem("w_split")
    stats_done = sem("stats_done")
    dve_self = sem("dve_self")
    pool_waits = sem("pool_waits")
    std_done = sem("std_done")
    v_filled = sem("v_filled")
    ctx_high = sem("ctx_high")
    ctx_split = sem("ctx_split")
    xn_done = sem("xn_done")
    piece_done = sem("piece_done")
    piece_high = sem("piece_high")
    piece_out = sem("piece_out")
    q_biased = sem("q_biased")
    q_masked = sem("q_masked")
    scores = sem("scores")
    max_done = sem("max_done")
    exp_done = sem("exp_done")
    inv_done = sem("inv_done")
    normed = sem("normed")
    flipped = sem("flipped")
    pT_done = sem("pT_done")
    pv_done = sem("pv_done")
    o_out = sem("o_out")
    sums_done = sem("sums_done")
    sums_out = sem("sums_out")
    proj_done = sem("proj_done")
    x_updated = sem("x_updated")

    SPLIT = [(wq_h, wq_l), (wk_h, wk_l), (wv_h, wv_l)]
    n_small = 2 + (4 if A.bias else 0)

    block = ctx.enter_context(nc.Block())

    @block.sync
    def _(sp):
        sp.dma_start(ctx_raw[:, :, :], dram["ctx"][0]).then_inc(ctx_loaded, 16)
        sp.dma_start(bo[:, :], dram["bo"]).then_inc(small_loaded, 16)
        sp.dma_start(wo[:, :, :], dram["wo"]).then_inc(small_loaded, 16)
        if A.bias:
            sp.dma_start(bq[:, :], dram["bq"]).then_inc(small_loaded, 16)
            sp.dma_start(bk[:, :], dram["bk"]).then_inc(small_loaded, 16)
            sp.dma_start(bv[:, :], dram["bv"]).then_inc(small_loaded, 16)
            sp.dma_start(head_mask[:, :, 0], dram["head_mask"]).then_inc(small_loaded, 16)
        first = 1
        if load_experts is not None:
            for b in range(1, E_N + 2):
                sp.wait_ge(ctx_split, b)
                sp.dma_start(ctx_raw[:, :, :], dram["ctx"][b]).then_inc(ctx_loaded, 16)
                load_experts(sp, b - 1)
            first = E_N + 2
        with sp.Fori(first, NB) as b:
            sp.wait_ge(ctx_split, b)
            sp.dma_start(ctx_raw[:, :, :], dram["ctx"][b]).then_inc(ctx_loaded, 16)

    @block.gpsimd
    def _(pool):
        def await_(sem_, value):
            if not (isinstance(value, int) and value <= 0):
                pool.wait_ge(sem_, value)
                pool.sem_inc(pool_waits, 1)

        def split_context(b):
            await_(ctx_loaded, b * 16 + 16)
            await_(piece_done, b * A.np)
            nc.gpsimd.tensor_copy(ctx_h[:, :], ctx_raw[:, 0, :])
            nc.gpsimd.tensor_copy(ctx_b[:, :], ctx_raw[:, 1, :]).then_inc(ctx_high, 1)
            pool.wait_ge(ctx_high, b * 2 + 1)
            nc.gpsimd.tensor_tensor(ctx_l[:, :], ctx_raw[:, 0, :], ctx_h[:, :].bitcast(F32), ALU.subtract)\
                .then_inc(ctx_high, 1)
            pool.wait_ge(ctx_high, b * 2 + 2)
            nc.gpsimd.tensor_tensor(ctx_b[64:128, :], ctx_raw[64:128, 1, :], ctx_b[64:128, :].bitcast(F32),
                                    ALU.subtract).then_inc(ctx_split, 1)
            await_(ctx_split, b + 1)

        nc.gpsimd.memset(v_sb[:, :, :, :], 1.0).then_inc(v_filled, 1)
        split_context(0)

        def mask_q(t, m):
            await_(piece_out, A.out(t, ("q", m)))
            for part, masked in ((q_h, qT_h), (q_l, qT_l)):
                last = nc.gpsimd.tensor_tensor(
                    masked[:, m, :, :], part[:, None, :].bitcast(F32).to_broadcast([128, A.variants, NQ]),
                    head_mask[:, :, :].to_broadcast([128, A.variants, NQ]), ALU.mult)
            last.then_inc(q_masked, 1)

        def double_q(t, m):
            await_(piece_out, A.out(t, ("q", m)))
            ms = slice(m * A.mq, (m + 1) * A.mq)
            for odd in range(2):
                mine, other = slice(64 * odd, 64 * odd + 64), slice(64 - 64 * odd, 128 - 64 * odd)
                nc.gpsimd.tensor_copy(q_twice[other, ms, odd, :], q_twice[mine, ms, odd, :]).then_inc(q_masked, 1)
                await_(q_masked, 4 * t + 2 * m + odd + 1)

        prepare_q = mask_q if A.bias else double_q
        for m in range(2):
            prepare_q(0, m)

        def step(b, h, prev, nxt):
            if h == A.split_at and nxt:
                split_context(b + 1)
            if nxt:
                for p in A.next_at.get(h, []):
                    if p[0] == "q":
                        prepare_q(b + 1, p[1])

        walk(pool, A.turn, step)

    @block.scalar
    def _(act):
        act.wait_ge(stats_done, 1)
        nc.scalar.activation(rstd[0:NQ, :], var[0:NQ, :], ACT.Sqrt).then_inc(std_done, 1)
        for n, (high, _) in enumerate(SPLIT):
            act.wait_ge(raw_loaded[n], 16)
            nc.scalar.copy(high[:, :, :], raw[:, n, :, :]).then_inc(w_high, 1)
        if A.bias:
            act.wait_ge(small_loaded, 16 * n_small)
        act.wait_ge(v_filled, 1)

        def piece_scalar(t, p):
            k = A.piece(p)
            src = p_ps[k % A.p_banks]
            if p[0] == "q" and A.bias:
                act.wait_ge(q_biased, t * 2 + p[1] + 1)
                wait(act, q_masked, t * 2 + p[1])
                nc.scalar.copy(q_h[:, :], q_t[:, :]).then_inc(piece_high, 1)
                return
            act.wait_ge(piece_done, t * A.np + k + 1)
            if p[0] == "x":
                nc.scalar.activation(xT_h[:, p[1], :], src[:, 0:NQ], ACT.Copy).then_inc(piece_high, 1)
            elif p[0] == "v":
                nc.scalar.activation(v_sb[0:KC, p[2], p[1] * A.vheads:(p[1] + 1) * A.vheads, 0:A.dh],
                                     src[0:KC, 0:A.vwide].rearrange("p (h d) -> p h d", d=A.dh), ACT.Copy)\
                    .then_inc(piece_high, 1)
            elif p[0] == "n":
                nc.scalar.activation(q_rows[0:NQ, p[1] * 512:(p[1] + 1) * 512], src[0:NQ, :], ACT.Copy,
                                     scale=A.scale).then_inc(piece_high, 1)
            elif p[0] == "q":
                ms = slice(p[1] * A.mq, (p[1] + 1) * A.mq)
                for odd in range(2):
                    rows = slice(64 * odd, 64 * odd + 64)
                    last = nc.scalar.activation(q_twice[rows, ms, odd, :],
                                                src[rows, 0:A.mq * NQ].rearrange("p (m q) -> p m q", q=NQ), ACT.Copy)
                last.then_inc(piece_high, 1)
            elif p[0] == "k" and A.bias:
                nc.scalar.activation(kT_h[:, p[1], :], src[:, 0:NKP], ACT.Identity,
                                     bias=bk[:, p[1]:p[1] + 1]).then_inc(piece_high, 1)
            elif p[0] == "k":
                for odd in range(2):
                    rows = slice(64 * odd, 64 * odd + 64)
                    last = nc.scalar.activation(k_both[rows, p[1], odd, :], src[rows, 0:NKP], ACT.Copy)
                last.then_inc(piece_high, 1)

        def exponent(b, h):
            act.wait_ge(max_done, b * H + h + 1)
            wait(act, flipped, b * H + h + 1 - P_RING)
            nc.scalar.activation(probs[0:NQ, h % P_RING, 0:NK], s_ps[S_BANK[h]][0:NQ, 0:NK], ACT.Exp,
                                 bias=nmax[0:NQ, h:h + 1], accum_out=rsum[0:NQ, h:h + 1]).then_inc(exp_done, 1)

        def take_flipped(b, h):
            act.wait_ge(flipped, b * H + h + 1)
            used = (h - PT_RING) // A.group + 1
            wait(act, pv_done, b * A.ngroups + (max(used, 0) if h >= A.turn else used))
            nc.scalar.copy(pT[0:KC, h % PT_RING, :], t_ps[h % T_BANKS][0:KC, 0:NC * NQ]).then_inc(pT_done, 1)

        def take_sums(b):
            act.wait_ge(sums_done, b + 1)
            wait(act, o_out, b)
            nc.scalar.copy(o_inv[:, :], y_ps[:, 0:O_BLOCKS * NQ]).then_inc(sums_out, 1)

        for p in A.before_out:
            if p in A.early:
                piece_scalar(0, p)
        for h in range(EXP_AHEAD):
            exponent(0, h)

        def step(b, h, prev, nxt):
            for p in A.this_out.get(h, []):
                if p in A.early:
                    piece_scalar(b, p)
            if nxt:
                for p in A.next_out.get(h, []):
                    if p in A.early:
                        piece_scalar(b + 1, p)
            if h + EXP_AHEAD < H:
                exponent(b, h + EXP_AHEAD)
            elif nxt:
                exponent(b + 1, h + EXP_AHEAD - H)
            take_flipped(b, h)
            if A.late_norm and h == 0 and prev:
                take_sums(b - 1)

        walk(act, A.turn, step)
        if A.late_norm:
            take_sums(NB - 1)

    @block.vector
    def _(dve):
        mine = [0]

        def link(ins):
            mine[0] += 1
            ins.then_inc(dve_self, 1)
            dve.wait_ge(dve_self, mine[0])

        for b in range(NB):
            last = nc.vector.bn_stats(stats[0:NQ, b, :], x_sb[0:NQ, b, :])
        link(last)
        for b in range(NB):
            last = nc.vector.bn_aggr(mv[0:NQ, b, :], stats[0:NQ, b, :])
        link(last)
        nc.vector.tensor_scalar(var[0:NQ, :], mv[0:NQ, :, 1], EPS, None, ALU.add).then_inc(stats_done, 1)
        for n, (high, low) in enumerate(SPLIT):
            dve.wait_ge(w_high, n + 1)
            nc.vector.tensor_tensor(low[:, :, :], raw[:, n, :, :], high[:, :, :].bitcast(F32),
                                    ALU.subtract).then_inc(w_split, 1)
            if n == 0:
                dve.wait_ge(std_done, 1)
                link(nc.vector.reciprocal(tmp[0:NQ, :], rstd[0:NQ, :]))
                link(nc.vector.tensor_tensor(rstd[0:NQ, :], tmp[0:NQ, :], tmp[0:NQ, :], ALU.mult))
                link(nc.vector.tensor_tensor(var[0:NQ, :], rstd[0:NQ, :], var[0:NQ, :], ALU.mult))
                link(nc.vector.tensor_scalar(var[0:NQ, :], var[0:NQ, :], -0.5, 1.5, ALU.mult, ALU.add))
                link(nc.vector.tensor_tensor(rstd[0:NQ, :], tmp[0:NQ, :], var[0:NQ, :], ALU.mult))
        dve.wait_ge(small_loaded, 16 * n_small)
        dve.wait_ge(v_filled, 1)

        def layernorm(b):
            if not isinstance(b, int) or b > 0:
                dve.wait_ge(piece_done, (b - 1) * A.np + A.piece(("x", 1)) + 1)
            nc.vector.tensor_scalar(xn[0:NQ, :], x_sb[0:NQ, bass.ds(b, 1), :].rearrange("p o d -> p (o d)"),
                                    mv[0:NQ, bass.ds(b, 1), 0], rstd[0:NQ, bass.ds(b, 1)],
                                    ALU.subtract, ALU.mult).then_inc(xn_done, 1)

        def piece_vector(t, p):
            if p not in A.late:
                return
            k = A.piece(p)
            src = p_ps[k % A.p_banks]
            if p[0] == "v":
                dve.wait_ge(piece_done, t * A.np + k + 1)
                out = v_sb[0:KC, p[2], p[1] * A.vheads:(p[1] + 1) * A.vheads, 0:A.dh]
                ins = src[0:KC, 0:A.vwide].rearrange("p (h d) -> p h d", d=A.dh)
                nc.vector.tensor_tensor(out, ins, bv[0:KC, :].rearrange("p (h d) -> p h d", d=A.dh),
                                        ALU.add).then_inc(piece_out, 1)
                return
            if p[0] == "q" and A.bias:
                m = p[1]
                dve.wait_ge(piece_done, t * A.np + k + 1)
                nc.vector.tensor_scalar(q_t[:, :], src[:, 0:NQ], bq[:, m:m + 1], A.scale, ALU.add, ALU.mult)\
                    .then_inc(q_biased, 1)
                dve.wait_ge(q_biased, t * 2 + m + 1)
                dve.wait_ge(piece_high, A.high(t, p))
                wait(dve, q_masked, t * 2 + m)
                nc.vector.tensor_tensor(q_l[:, :], q_t[:, :], q_h[:, :].bitcast(F32), ALU.subtract)\
                    .then_inc(piece_out, 1)
                return
            dve.wait_ge(piece_high, A.high(t, p))
            if p[0] == "x":
                nc.vector.tensor_tensor(xT_l[:, p[1], :], src[:, 0:NQ], xT_h[:, p[1], :].bitcast(F32),
                                        ALU.subtract).then_inc(piece_out, 1)
            elif p[0] == "q":
                ms = slice(p[1] * A.mq, (p[1] + 1) * A.mq)
                for odd in range(2):
                    rows = slice(64 * odd, 64 * odd + 64)
                    last = nc.vector.tensor_tensor(
                        qT_l[rows, ms, 0, :], src[rows, 0:A.mq * NQ].rearrange("p (m q) -> p m q", q=NQ),
                        q_twice[rows, ms, odd, :].bitcast(F32), ALU.subtract)
                last.then_inc(piece_out, 1)
            elif A.bias:
                nc.vector.scalar_tensor_tensor(
                    out=kT_l[:, p[1], :], in0=src[:, 0:NKP], scalar=bk[:, p[1]:p[1] + 1],
                    in1=kT_h[:, p[1], :].bitcast(F32), op0=ALU.add, op1=ALU.subtract).then_inc(piece_out, 1)
            else:
                for odd in range(2):
                    rows, other = slice(64 * odd, 64 * odd + 64), slice(64 - 64 * odd, 128 - 64 * odd)
                    last = nc.vector.tensor_tensor(k_both[other, p[1], odd, :], src[rows, 0:NKP],
                                                   k_both[rows, p[1], odd, :].bitcast(F32), ALU.subtract)
                last.then_inc(piece_out, 1)

        def row_max(b, h):
            dve.wait_ge(scores, b * H + h + 1)
            nc.vector.tensor_reduce(nmax[0:NQ, h:h + 1], s_ps[S_BANK[h]][0:NQ, 0:NK], AX.X, ALU.max, negate=True)\
                .then_inc(max_done, 1)

        def normalise(b, h):
            if A.late_norm:
                return
            dve.wait_ge(exp_done, b * H + h + 1)
            nc.vector.reciprocal(rinv[0:NQ, h:h + 1], rsum[0:NQ, h:h + 1]).then_inc(inv_done, 1)
            dve.wait_ge(inv_done, b * H + h + 1)
            p = probs[0:NQ, h % P_RING, 0:NK]
            nc.vector.tensor_scalar(p, p, rinv[0:NQ, h:h + 1], None, ALU.mult).then_inc(normed, 1)

        def invert_sums(b, g):
            dve.wait_ge(exp_done, b * H + (g + 1) * A.group)
            if g == 0:
                wait(dve, sums_done, b)
            heads = slice(g * A.group, (g + 1) * A.group)
            nc.vector.reciprocal(rinv[0:NQ, heads], rsum[0:NQ, heads]).then_inc(inv_done, 1)
            dve.wait_ge(inv_done, 2 * (b * A.ngroups + g) + 1)
            nc.vector.tensor_copy(inv_wide[0:NQ, heads, :], rinv[0:NQ, heads, None].to_broadcast([NQ, A.group, A.vw]))\
                .then_inc(inv_done, 1)

        def take_output(b, half):
            dve.wait_ge(pv_done, b * A.ngroups + O_BLOCKS * (half + 1))
            out = oT[:, half * O_BLOCKS:(half + 1) * O_BLOCKS, :]
            ins = o_ps[:, 0:O_BLOCKS * NQ].rearrange("p (g q) -> p g q", q=NQ)
            if A.late_norm:
                dve.wait_ge(sums_out, b + 1)
                nc.vector.tensor_tensor(out, ins, o_inv[:, :].rearrange("p (g q) -> p g q", q=NQ), ALU.mult)\
                    .then_inc(o_out, 1)
            else:
                nc.vector.tensor_copy(out, ins).then_inc(o_out, 1)

        def update_x(b):
            dve.wait_ge(proj_done, b + 1)
            nc.vector.tensor_tensor(y_sb[0:NQ, :], y_ps[0:NQ, 0:D], bo[0:NQ, :], ALU.add).then_inc(x_updated, 1)
            dve.wait_ge(x_updated, 2 * b + 1)
            xb = x_sb[0:NQ, bass.ds(b, 1), :].rearrange("p o d -> p (o d)")
            nc.vector.scalar_tensor_tensor(out=xb, in0=y_sb[0:NQ, :], scalar=tg[0:NQ, tg_col:tg_col + 1],
                                           in1=xb, op0=ALU.mult, op1=ALU.add).then_inc(x_updated, 1)

        layernorm(0)
        for p in A.before_out:
            piece_vector(0, p)
        for h in range(MAX_AHEAD):
            row_max(0, h)
        normalise(0, 0)

        def step(b, h, prev, nxt):
            if h == 5 and nxt:
                layernorm(b + 1)
            if h + 1 < H:
                normalise(b, h + 1)
            elif nxt:
                normalise(b + 1, 0)
            if h == 2 and prev:
                take_output(b - 1, A.nout - 1)
            if A.nout == 2 and h == A.pv_step(O_BLOCKS - 1) + 1:
                take_output(b, 0)
            if h == A.project_at + 1 and prev:
                update_x(b - 1)
            for p in A.this_out.get(h, []):
                piece_vector(b, p)
            if nxt:
                for p in A.next_out.get(h, []):
                    piece_vector(b + 1, p)
            if h + MAX_AHEAD < H:
                row_max(b, h + MAX_AHEAD)
            elif nxt:
                row_max(b + 1, h + MAX_AHEAD - H)
            if A.late_norm and h % A.group == A.group - 1:
                invert_sums(b, h // A.group)

        walk(dve, A.turn, step)
        take_output(NB - 1, A.nout - 1)
        update_x(NB - 1)

    @block.tensor
    def _(pe):
        def products(out, terms):
            for n, (a, b) in enumerate(terms):
                last = nc.tensor.matmul(out, a, b, start=(n == 0), stop=(n == len(terms) - 1))
            return last

        def await_taken(t, p):
            if p in A.late:
                pe.wait_ge(piece_out, A.out(t, p))
            else:
                pe.wait_ge(piece_high, A.high(t, p))

        def piece_tensor(t, p):
            k = A.piece(p)
            dst = p_ps[k % A.p_banks]
            before = A.order[k - A.p_banks]
            t_before = t - 1 if k < A.p_banks else t
            if not (isinstance(t_before, int) and t_before < 0):
                await_taken(t_before, before)
            if not A.bias and p == A.behind_y:
                wait(pe, x_updated, 2 * t - 1)
            if p[0] == "x":
                pe.wait_ge(xn_done, t + 1)
                nc.tensor.transpose(dst[:, 0:NQ], xn[0:NQ, p[1] * 128:(p[1] + 1) * 128],
                                    ident[0:NQ, 0:NQ]).then_inc(piece_done, 1)
            elif p[0] == "n":
                pe.wait_ge(piece_out, A.out(t, ("x", 1)))
                cols = slice(p[1] * 512, (p[1] + 1) * 512)
                products(dst[0:NQ, :], [
                    t_ for c in range(2) for t_ in (
                        (xT_h[:, c, :], wq_h[:, c, cols]), (xT_h[:, c, :], wq_l[:, c, cols]),
                        (xT_l[:, c, :], wq_h[:, c, cols]))]).then_inc(piece_done, 1)
            elif p[0] == "q" and not A.bias:
                pe.wait_ge(piece_high, A.high(t, ("n", p[1])))
                for n in range(A.mq):
                    cols = slice((p[1] * A.mq + n) * 128, (p[1] * A.mq + n + 1) * 128)
                    last = nc.tensor.transpose(dst[:, n * NQ:(n + 1) * NQ], q_rows[0:NQ, cols], ident[0:NQ, 0:NQ])
                last.then_inc(piece_done, 1)
            elif p[0] == "q":
                pe.wait_ge(piece_out, A.out(t, ("x", 1)))
                for n in range(A.mq):
                    cols = slice((p[1] * A.mq + n) * 128, (p[1] * A.mq + n + 1) * 128)
                    last = products(dst[:, n * NQ:(n + 1) * NQ], [
                        t_ for c in range(2) for t_ in (
                            (wq_h[:, c, cols], xT_h[:, c, :]), (wq_h[:, c, cols], xT_l[:, c, :]),
                            (wq_l[:, c, cols], xT_h[:, c, :]))])
                last.then_inc(piece_done, 1)
            elif p[0] == "k":
                pe.wait_ge(ctx_split, t + 1)
                cols = slice(p[1] * 128, (p[1] + 1) * 128)
                products(dst[:, 0:NKP], [
                    (wk_h[:, 0, cols], ctx_h[:, :]), (wk_h[:, 0, cols], ctx_l[:, :]),
                    (wk_l[:, 0, cols], ctx_h[:, :]),
                    (wk_h[:, 1, cols], ctx_b[:, :]),
                    (wk_l[0:64, 1, cols], ctx_b[0:64, :])]).then_inc(piece_done, 1)
            else:
                pe.wait_ge(ctx_split, t + 1)
                cols = slice(p[1] * A.vwide, (p[1] + 1) * A.vwide)
                keys = slice(p[2] * KC, (p[2] + 1) * KC)
                products(dst[0:KC, 0:A.vwide], [
                    (ctx_h[:, keys], wv_h[:, 0, cols]), (ctx_h[:, keys], wv_l[:, 0, cols]),
                    (ctx_l[:, keys], wv_h[:, 0, cols]),
                    (ctx_b[:, keys], wv_h[:, 1, cols]),
                    (ctx_b[0:64, keys], wv_l[0:64, 1, cols])]).then_inc(piece_done, 1)

        def score(b, h):
            pe.wait_ge(piece_out, A.out(b, A.scores_need(h)))
            wait(pe, exp_done, b * H + h + 1 - S_BACK[h])
            m, r = h // A.hpt, h % A.hpt
            if A.bias:
                pe.wait_ge(q_masked, b * 2 + m + 1)
                terms = [(qT_h[:, m, r, :], kT_h[:, m, :]), (qT_h[:, m, r, :], kT_l[:, m, :]),
                         (qT_l[:, m, r, :], kT_h[:, m, :])]
            else:
                pe.wait_ge(q_masked, b * 4 + 2 * (h // (H // 2)) + 2)
                rows = slice(64 * r, 64 * r + 64)
                terms = [(q_twice[:, m, r, :], k_both[:, m, r, :]), (qT_l[rows, m, 0, :], k_both[rows, m, r, :])]
            products(s_ps[S_BANK[h]][0:NQ, 0:NKP], terms).then_inc(scores, 1)

        def flip(b, h):
            pe.wait_ge(exp_done if A.late_norm else normed, b * H + h + 1)
            wait(pe, pT_done, b * H + h + 1 - T_BANKS)
            for c in range(NC):
                last = nc.tensor.transpose(t_ps[h % T_BANKS][0:KC, c * NQ:(c + 1) * NQ],
                                           probs[0:NQ, h % P_RING, c * KC:(c + 1) * KC], ident[0:NQ, 0:NQ])
            last.then_inc(flipped, 1)

        def weigh(b, g):
            pe.wait_ge(pT_done, b * H + (g + 1) * A.group)
            await_taken(b, A.last_v[g * A.group // A.vheads])
            if g % O_BLOCKS == 0:
                if g:
                    pe.wait_ge(o_out, b * A.nout + 1)
                else:
                    wait(pe, o_out, b * A.nout)
            q0 = (g % O_BLOCKS) * NQ
            for c in range(NC):
                for j in range(A.group):
                    h = g * A.group + j
                    last = nc.tensor.matmul(o_ps[A.vw * j:A.vw * (j + 1), q0:q0 + NQ], v_sb[0:KC, c, h, :],
                                            pT[0:KC, h % PT_RING, c * NQ:(c + 1) * NQ],
                                            start=(c == 0), stop=(c == NC - 1))
            last.then_inc(pv_done, 1)

        def spread_sums(b):
            pe.wait_ge(inv_done, 2 * (b + 1) * A.ngroups)
            wait(pe, x_updated, 2 * b)
            for g in range(A.ngroups):
                last = nc.tensor.transpose(
                    y_ps[:, g * NQ:(g + 1) * NQ],
                    inv_wide[0:NQ, g * A.group:(g + 1) * A.group, :].rearrange("p h d -> p (h d)"),
                    ident[0:NQ, 0:NQ])
            last.then_inc(sums_done, 1)

        def project(b):
            pe.wait_ge(o_out, (b + 1) * A.nout)
            if A.late_norm:
                pe.wait_ge(sums_out, b + 1)
            elif isinstance(b, int) and b == NB - 1:
                await_taken(NB - 1, A.order[-1])
                await_taken(NB - 1, A.order[-2])
            else:
                await_taken(b + 1, A.order[A.piece(A.behind_y) - A.p_banks])
            products(y_ps[0:NQ, 0:D], [(oT[:, g, :], wo[:, g, :]) for g in range(A.ngroups)])\
                .then_inc(proj_done, 1)

        pe.wait_ge(w_split, 3)
        pe.wait_ge(small_loaded, 16 * n_small)
        for p in A.before:
            piece_tensor(0, p)
        for h in range(S_AHEAD):
            score(0, h)

        def step(b, h, prev, nxt):
            if h + S_AHEAD < H:
                score(b, h + S_AHEAD)
            elif nxt:
                score(b + 1, h + S_AHEAD - H)
            flip(b, h)
            for g in range(A.ngroups):
                if A.pv_step(g) == h:
                    weigh(b, g)
                elif A.pv_step(g) == h + H and prev:
                    weigh(b - 1, g)
            for p in A.this_at.get(h, []):
                piece_tensor(b, p)
            if nxt:
                for p in A.next_at.get(h, []):
                    piece_tensor(b + 1, p)
            if A.late_norm and h == 0 and prev:
                spread_sums(b - 1)
            if h == A.project_at and prev:
                project(b - 1)

        walk(pe, A.turn, step)
        if A.late_norm:
            spread_sums(NB - 1)
        for g in range(A.ngroups):
            if A.pv_step(g) >= H:
                weigh(NB - 1, g)
        project(NB - 1)

    ctx.close()


E_N = 8
TOKENS = NB * NQ
ROWS = 128
SH_TILES = TOKENS // ROWS
RT_TILES = (2 * TOKENS + E_N * (ROWS - 1)) // ROWS
F0 = 512
F1 = 1024
CAP = 280
FAR = 1 << 20


def routing(nc, keep, R, x_sb, ident, consts, dram, prefetch=None):
    ctx = ExitStack()
    T = R["tag"]

    def sb(name, shape, dt=F32):
        return ctx.enter_context(nc.sbuf_tensor(f"{T}_{name}", shape, dt))

    def sem(name):
        return keep.enter_context(nc.semaphore(f"{T}_{name}"))

    xn, scat = R["xn"], R["scatter_to"]
    xT = sb("xT", [128, 2, 2, NQ])
    gw = sb("gw", [128, 2, E_N])
    gb = sb("gb", [128, E_N])
    stats, mv = sb("stats", [128, NB, 6]), sb("mv", [128, NB, 2])
    var, std, inv, tmp = (sb(n, [128, NB]) for n in ("var", "std", "inv", "tmp"))
    S3 = [128, NB, E_N]
    logit, shifted, ex, top0, top1, both, within, before, slots, picked = (
        sb(n, S3) for n in ("logit", "shifted", "ex", "top0", "top1", "both", "within", "before", "slots", "picked"))
    total = sb("total", S3)
    run = [sb(f"run{n}", [128, NB + 8, E_N]) for n in range(2)]
    rank4, tie4 = sb("rank4", [128, NB, E_N, E_N]), sb("tie4", [128, NB, E_N, E_N])
    most, den, rden = (sb(n, [128, NB]) for n in ("most", "den", "rden"))
    need14 = sb("need14", [128, E_N, SH_TILES])
    etile = [sb(f"etile{n}", [128, 4 + E_N]) for n in range(2)]
    ntile = sb("ntile", [128, E_N])
    late = sb("late", [128, RT_TILES, E_N])
    tab_f = sb("tab_f", [128, RT_TILES])
    slot_f, have = sb("slot_f", [128, 2, NB]), sb("have", [128, 2, NB])

    t_ps = [ctx.enter_context(nc.psum_tensor(f"{T}_t_ps{n}", [128, 2, 256], F32)) for n in range(2)]
    l_ps = ctx.enter_context(nc.psum_tensor(f"{T}_l_ps", [128, 512], F32))
    c_ps = ctx.enter_context(nc.psum_tensor(f"{T}_c_ps", [128, 2, 256], F32))

    loaded, stats_done, std_done = sem("loaded"), sem("stats_done"), sem("std_done")
    xn_done, flipped, xT_out, gated = sem("xn_done"), sem("flipped"), sem("xT_out"), sem("gated")
    shifted_done, exp_done, chosen, counted = sem("shifted_done"), sem("exp_done"), sem("chosen"), sem("counted")
    dve_self, slots_done = sem("dve_self"), sem("slots_done")
    copied = sem("copied")
    layer = R["layer"]
    block = ctx.enter_context(nc.Block())

    @block.sync
    def _(sp):
        sp.dma_start(gw[:, :, :], dram["gw"]).then_inc(loaded, 16)
        if prefetch is not None:
            prefetch(sp)
        if layer == 1:
            sp.dma_start(gb[:, :], dram["gb"]).then_inc(loaded, 16)
        else:
            shared = R["rows"][0:TOKENS, :].rearrange("(b p) d -> p b d", p=NQ)
            sp.wait_ge(xn_done, NB)
            sp.dma_start(shared, xn[0:NQ, :, :]).then_inc(copied, 16)
            sp.wait_ge(copied, 16)

    @block.scalar
    def _(act):
        act.wait_ge(stats_done, 1)
        nc.scalar.activation(std[0:NQ, :], var[0:NQ, :], ACT.Sqrt).then_inc(std_done, 1)
        for b in range(NB):
            act.wait_ge(flipped, b + 1)
            if b >= 2:
                act.wait_ge(gated, b - 1)
            nc.scalar.copy(xT[:, b % 2, :, :], t_ps[b % 2][:, :, 0:NQ]).then_inc(xT_out, 1)
        act.wait_ge(shifted_done, 1)
        nc.scalar.activation(ex[0:NQ, :, :], shifted[0:NQ, :, :], ACT.Exp).then_inc(exp_done, 1)

    @block.tensor
    def _(pe):
        def gate(b):
            pe.wait_ge(xT_out, b + 1)
            for c in range(2):
                last = nc.tensor.matmul(l_ps[0:NQ, b * E_N:(b + 1) * E_N], xT[:, b % 2, c, :], gw[:, c, :],
                                        start=(c == 0), stop=(c == 1))
            last.then_inc(gated, 1)

        pe.wait_ge(loaded, 16 * (1 + layer))
        for b in range(NB):
            pe.wait_ge(xn_done, b + 1)
            if b >= 2:
                pe.wait_ge(xT_out, b - 1)
            for c in range(2):
                last = nc.tensor.transpose(t_ps[b % 2][:, c, 0:NQ], xn[0:NQ, b, c * 128:(c + 1) * 128],
                                           ident[0:NQ, 0:NQ])
            last.then_inc(flipped, 1)
            if b:
                gate(b - 1)
        gate(NB - 1)
        pe.wait_ge(chosen, 1)
        flat = both[0:NQ, :, :].rearrange("p b e -> p (b e)")
        nc.tensor.matmul(c_ps[0:NQ, 0, 0:NB * E_N], consts["earlier"][0:NQ, 0:NQ], flat, start=True, stop=True)
        nc.tensor.matmul(c_ps[0:NQ, 1, 0:NB * E_N], consts["ones"][0:NQ, 0:NQ], flat, start=True, stop=True)\
            .then_inc(counted, 1)

    @block.vector
    def _(dve):
        mine = [0]

        def link(ins):
            mine[0] += 1
            ins.then_inc(dve_self, 1)
            dve.wait_ge(dve_self, mine[0])

        q = slice(0, NQ)
        tt, ts = nc.vector.tensor_tensor, nc.vector.tensor_scalar
        for n in range(2):
            nc.vector.memset(run[n][:, :, :], 0.0)
            last = nc.vector.memset(etile[n][:, :], 0.0)
        link(last)
        for b in range(NB):
            last = nc.vector.bn_stats(stats[q, b, :], x_sb[q, b, :])
        link(last)
        for b in range(NB):
            last = nc.vector.bn_aggr(mv[q, b, :], stats[q, b, :])
        link(last)
        ts(var[q, :], mv[q, :, 1], EPS, None, ALU.add).then_inc(stats_done, 1)
        dve.wait_ge(std_done, 1)
        link(nc.vector.reciprocal(tmp[q, :], std[q, :]))
        link(tt(inv[q, :], tmp[q, :], tmp[q, :], ALU.mult))
        link(tt(inv[q, :], inv[q, :], var[q, :], ALU.mult))
        link(ts(inv[q, :], inv[q, :], -0.5, 1.5, ALU.mult, ALU.add))
        link(tt(inv[q, :], inv[q, :], tmp[q, :], ALU.mult))
        for b in range(NB):
            ts(xn[q, b, :], x_sb[q, b, :], mv[q, b, 0:1], inv[q, b:b + 1], ALU.subtract, ALU.mult).then_inc(xn_done, 1)
        dve.wait_ge(gated, NB)
        dve.wait_ge(loaded, 16 * (1 + layer))
        gates = l_ps[q, 0:NB * E_N].rearrange("p (b e) -> p b e", e=E_N)
        if layer == 1:
            link(tt(logit[q, :, :], gates, gb[q, None, :].to_broadcast([NQ, NB, E_N]), ALU.add))
        else:
            link(nc.vector.tensor_copy(logit[q, :, :], gates))
        link(nc.vector.tensor_reduce(most[q, :], logit[q, :, :], AX.X, ALU.max))
        tt(shifted[q, :, :], logit[q, :, :], most[q, :, None].to_broadcast([NQ, NB, E_N]), ALU.subtract)\
            .then_inc(shifted_done, 1)
        other = logit[q, :, None, :].to_broadcast([NQ, NB, E_N, E_N])
        own = logit[q, :, :, None].to_broadcast([NQ, NB, E_N, E_N])
        tt(rank4[q], other, own, ALU.is_gt)
        link(tt(tie4[q], other, own, ALU.is_equal))
        link(tt(tie4[q], tie4[q], consts["before"][q, None, :, :].to_broadcast([NQ, NB, E_N, E_N]), ALU.mult))
        link(tt(rank4[q], rank4[q], tie4[q], ALU.add))
        link(nc.vector.tensor_reduce(picked[q, :, :], rank4[q], AX.X, ALU.add))
        ts(top0[q, :, :], picked[q, :, :], 0.0, None, ALU.is_equal)
        link(ts(top1[q, :, :], picked[q, :, :], 1.0, None, ALU.is_equal))
        dve.wait_ge(exp_done, 1)
        if layer == 1:
            link(nc.vector.tensor_reduce(den[q, :], ex[q, :, :], AX.X, ALU.add))
            link(nc.vector.reciprocal(rden[q, :], den[q, :]))
            link(tt(ex[q, :, :], ex[q, :, :], rden[q, :, None].to_broadcast([NQ, NB, E_N]), ALU.mult))
            link(ts(both[q, :, :], ex[q, :, :], 0.0, None, ALU.is_gt))
            tt(top0[q, :, :], top0[q, :, :], both[q, :, :], ALU.mult)
            link(tt(top1[q, :, :], top1[q, :, :], both[q, :, :], ALU.mult))
            tt(both[q, :, :], top0[q, :, :], top1[q, :, :], ALU.add).then_inc(chosen, 1)
        else:
            tt(both[q, :, :], top0[q, :, :], top1[q, :, :], ALU.add).then_inc(chosen, 1)
            dve.wait_ge(chosen, 1)
            link(tt(ex[q, :, :], ex[q, :, :], both[q, :, :], ALU.mult))
            link(nc.vector.tensor_reduce(den[q, :], ex[q, :, :], AX.X, ALU.add))
            link(nc.vector.reciprocal(rden[q, :], den[q, :]))
            link(tt(ex[q, :, :], ex[q, :, :], rden[q, :, None].to_broadcast([NQ, NB, E_N]), ALU.mult))
        dve.wait_ge(counted, 1)
        mid = slice(8, 8 + NB)
        nc.vector.tensor_copy(within[q, :, :], c_ps[q, 0, 0:NB * E_N].rearrange("p (b e) -> p b e", e=E_N))
        link(nc.vector.tensor_copy(total[q, :, :], c_ps[q, 1, 0:NB * E_N].rearrange("p (b e) -> p b e", e=E_N)))
        link(nc.vector.tensor_copy(run[0][q, mid, :], total[q, :, :]))
        for n, k in enumerate((1, 2, 4, 8)):
            a, z = run[n % 2], run[(n + 1) % 2]
            link(tt(z[q, mid, :], a[q, mid, :], a[q, 8 - k:8 - k + NB, :], ALU.add))
        link(tt(before[q, :, :], run[0][q, mid, :], total[q, :, :], ALU.subtract))
        link(tt(slots[q, :, :], within[q, :, :], before[q, :, :], ALU.add))
        if layer == 1:
            link(ts(picked[q, :, :], slots[q, :, :], float(CAP), None, ALU.is_lt))
            tt(top0[q, :, :], top0[q, :, :], picked[q, :, :], ALU.mult)
            tt(top1[q, :, :], top1[q, :, :], picked[q, :, :], ALU.mult)
            link(tt(slots[q, :, :], slots[q, :, :],
                    consts["list_at"][q, None, :].to_broadcast([NQ, NB, E_N]), ALU.add))
        else:
            link(tt(need14[q], run[0][q, 8 + NB - 1, :, None].to_broadcast([NQ, E_N, SH_TILES]),
                    consts["tile_rows"][q, None, 0:SH_TILES].to_broadcast([NQ, E_N, SH_TILES]), ALU.is_gt))
            link(nc.vector.tensor_reduce(ntile[q, :], need14[q], AX.X, ALU.add))
            link(nc.vector.tensor_copy(etile[0][q, 4:], ntile[q, :]))
            for n, k in enumerate((1, 2, 4)):
                a, z = etile[n % 2], etile[(n + 1) % 2]
                link(tt(z[q, 4:], a[q, 4:], a[q, 4 - k:4 - k + E_N], ALU.add))
            ends = etile[1]
            link(tt(late[q], consts["tile_no"][q, 0:RT_TILES, None].to_broadcast([NQ, RT_TILES, E_N]),
                    ends[q, None, 4:].to_broadcast([NQ, RT_TILES, E_N]), ALU.is_ge))
            link(nc.vector.tensor_reduce(tab_f[q, :], late[q], AX.X, ALU.add))
            link(ts(tab_f[q, :], tab_f[q, :], float(E_N - 1), None, ALU.min))
            nc.vector.tensor_copy(R["table"][q, :], tab_f[q, :])
            link(tt(ntile[q, :], ends[q, 4:], ntile[q, :], ALU.subtract))
            link(ts(ntile[q, :], ntile[q, :], float(ROWS), float(R["first"]), ALU.mult, ALU.add))
            link(tt(slots[q, :, :], slots[q, :, :], ntile[q, None, :].to_broadcast([NQ, NB, E_N]), ALU.add))
        for k, top in enumerate((top0, top1)):
            link(nc.vector.tensor_reduce(have[q, k, :], top[q, :, :], AX.X, ALU.add))
            link(tt(picked[q, :, :], top[q, :, :], slots[q, :, :], ALU.mult))
            link(nc.vector.tensor_reduce(slot_f[q, k, :], picked[q, :, :], AX.X, ALU.add))
            link(tt(picked[q, :, :], top[q, :, :], ex[q, :, :], ALU.mult))
            link(nc.vector.tensor_reduce(R["weight"][q, k, :], picked[q, :, :], AX.X, ALU.add))
        link(nc.vector.tensor_copy(R["slot"][q], slot_f[q]))
        ts(R["weight"][q], R["weight"][q], R["tg"][q], None, ALU.mult)
        link(ts(have[q], have[q], -float(FAR), float(FAR), ALU.mult, ALU.add))
        link(tt(slot_f[q], slot_f[q], have[q], ALU.add))
        nc.vector.tensor_copy(scat[q], slot_f[q]).then_inc(slots_done, 1)

    ctx.close()


def scatter_rows(nc, R, scattered):
    for b in range(NB):
        for k in range(2):
            nc.gpsimd.indirect_dma_start(
                out=R["rows"], out_offset=bass.IndirectOffsetOnAxis(ap=R["scatter_to"][0:NQ, k, b:b + 1], axis=0),
                in_=R["xn"][0:NQ, b, :], in_offset=None, bounds_check=R["rows"].shape[0] - 1,
                oob_is_err=False).then_inc(scattered, 16)


SCATTERED = 16 * 2 * NB


def pairs(eng, first, start, stop, step):
    assert (start - first) % 2 == 0 and (stop - start) % 2 == 0
    with eng.Fori(start // 2, stop // 2) as i:
        step(i, 0)
        step(i, 1)


def experts0(nc, keep, R, w12, w3, w_loaded, rows_out, ident, prefetch):
    ctx = ExitStack()
    rows_in, table = R["rows"], R["table"]

    def sb(name, shape, dt=F32):
        return ctx.enter_context(nc.sbuf_tensor(f"e0_{name}", shape, dt))

    def sem(name):
        return keep.enter_context(nc.semaphore(f"e0_{name}"))

    xg = sb("xg", [128, 2, D])
    xT = sb("xT", [128, 2, 2, ROWS])
    s, g = sb("s", [128, 2, F0]), sb("g", [128, 2, F0])
    gT = sb("gT", [128, 2, 4, ROWS])
    y = sb("y", [128, 2, D])
    h1 = [ctx.enter_context(nc.psum_tensor(f"e0_h1_{n}", [128, F0], F32)) for n in range(2)]
    h2 = [ctx.enter_context(nc.psum_tensor(f"e0_h2_{n}", [128, F0], F32)) for n in range(2)]
    gT_ps = [ctx.enter_context(nc.psum_tensor(f"e0_gT_ps{n}", [128, 4, ROWS], F32)) for n in range(2)]
    xT_ps = ctx.enter_context(nc.psum_tensor("e0_xT_ps", [128, 4, ROWS], F32))
    y_ps = ctx.enter_context(nc.psum_tensor("e0_y_ps", [128, 2, D], F32))
    xg_loaded = [sem(f"xg_loaded{n}") for n in range(2)]
    stored = [sem(f"stored{n}") for n in range(2)]
    x_flipped, xT_out, h_done, s_done, g_done = (sem(n) for n in ("x_flipped", "xT_out", "h_done", "s_done", "g_done"))
    g_flipped, gT_out, y_done, y_out = (sem(n) for n in ("g_flipped", "gT_out", "y_done", "y_out"))
    scattered = sem("scattered")
    NT = SH_TILES + RT_TILES
    in_v = rows_in.rearrange("(t p) d -> t p d", p=ROWS)
    out_v = rows_out.rearrange("(t p) d -> t p d", p=ROWS)
    assert NT % 2 == 1 and SH_TILES % 2 == 0

    def tiles(eng, step):
        for n in range(2):
            step(0, n, 2)
        with eng.Fori(1, SH_TILES // 2 - 1) as i:
            step(i, 0, 2)
            step(i, 1, 2)
        for n in range(2):
            step(SH_TILES // 2 - 1, n, 2)
        with eng.Fori(SH_TILES // 2, NT // 2 - 1) as i:
            step(i, 0, 2)
            step(i, 1, 2)
        step(NT // 2 - 1, 0, 2)
        step(NT // 2 - 1, 1, 1)
        step(NT // 2, 0, 0)

    block = ctx.enter_context(nc.Block())

    @block.sync
    def _(sp):
        def load(i, n):
            if isinstance(i, int) and 2 * i + n == SH_TILES:
                sp.wait_ge(scattered, SCATTERED)
            wait(sp, x_flipped, 2 * i + n - 1)
            sp.dma_start(xg[:, n, :], in_v[2 * i + n]).then_inc(xg_loaded[n], 16)

        load(0, 0)
        load(0, 1)
        prefetch(sp)

        def step(i, n, ahead):
            if ahead == 2:
                load(i + 1, n)
            sp.wait_ge(y_out, 2 * i + n + 1)
            sp.dma_start(out_v[2 * i + n], y[:, n, :]).then_inc(stored[n], 16)

        tiles(sp, step)
        sp.wait_ge(stored[0], 16 * (NT // 2 + 1))
        sp.wait_ge(stored[1], 16 * (NT // 2))

    @block.gpsimd
    def _(pool):
        scatter_rows(nc, R, scattered)
        pool.wait_ge(scattered, SCATTERED)

    @block.tensor
    def _(pe):
        def flip_x(i, n):
            pe.wait_ge(xg_loaded[n], 16 * (i + 1))
            wait(pe, xT_out, 2 * i + n)
            for c in range(2):
                last = nc.tensor.transpose(xT_ps[:, c, :], xg[:, n, c * 128:(c + 1) * 128], ident[:, :])
            last.then_inc(x_flipped, 1)

        def hidden(i, n, e):
            pe.wait_ge(xT_out, 2 * i + n + 1)
            wait(pe, g_done, 2 * i + n - 1)
            for j, bank in enumerate((h1[n], h2[n])):
                for c in range(2):
                    last = nc.tensor.matmul(bank[:, :], xT[:, n, c, :],
                                            w12[:, bass.ds(e * (4 * F0) + (2 * j + c) * F0, F0)],
                                            start=(c == 0), stop=(c == 1))
            last.then_inc(h_done, 1)

        def flip_g(i, n):
            pe.wait_ge(g_done, 2 * i + n + 1)
            wait(pe, gT_out, 2 * i + n - 1)
            for k in range(4):
                last = nc.tensor.transpose(gT_ps[n][:, k, :], g[:, n, k * 128:(k + 1) * 128], ident[:, :])
            last.then_inc(g_flipped, 1)

        def output(i, n, e):
            pe.wait_ge(gT_out, 2 * i + n + 1)
            wait(pe, y_out, 2 * i + n)
            for k in range(4):
                last = nc.tensor.matmul(y_ps[:, 0, :], gT[:, n, k, :], w3[:, bass.ds(e * (4 * D) + k * D, D)],
                                        start=(k == 0), stop=(k == 3))
            last.then_inc(y_done, 1)

        def expert(i, n):
            if isinstance(i, int) and 2 * i + n < SH_TILES:
                return E_N
            return pe.value_load(table[0:1, bass.ds(2 * i + n - SH_TILES, 1)], min_val=0, max_val=E_N - 1)

        pe.wait_ge(w_loaded, 32 * (E_N + 1))
        flip_x(0, 0)
        flip_x(0, 1)
        hidden(0, 0, E_N)

        def one(i, n, ahead, mine, next_):
            flip_g(i, n)
            if ahead:
                hidden(*((i, 1) if n == 0 else (i + 1, 0)), next_)
            if ahead == 2:
                flip_x(i + 1, n)
            output(i, n, mine)

        def routed_pair(i, last):
            e = [expert(i, 0), expert(i, 1), expert(i + 1, 0)]
            one(i, 0, 2, e[0], e[1])
            one(i, 1, 1 if last else 2, e[1], e[2])

        for n in range(2):
            one(0, n, 2, E_N, E_N)
        with pe.Fori(1, SH_TILES // 2 - 1) as i:
            one(i, 0, 2, E_N, E_N)
            one(i, 1, 2, E_N, E_N)
        one(SH_TILES // 2 - 1, 0, 2, E_N, E_N)
        one(SH_TILES // 2 - 1, 1, 2, E_N, expert(SH_TILES // 2, 0))
        with pe.Fori(SH_TILES // 2, NT // 2 - 1) as i:
            routed_pair(i, False)
        routed_pair(NT // 2 - 1, True)
        one(NT // 2, 0, 0, expert(NT // 2, 0), None)

    @block.scalar
    def _(act):
        def take_x(i, n):
            act.wait_ge(x_flipped, 2 * i + n + 1)
            wait(act, h_done, 2 * i + n - 1)
            nc.scalar.copy(xT[:, n, :, :], xT_ps[:, 0:2, :]).then_inc(xT_out, 1)

        def silu(i, n):
            act.wait_ge(h_done, 2 * i + n + 1)
            wait(act, g_done, 2 * i + n - 1)
            nc.scalar.activation(s[:, n, :], h1[n][:, :], ACT.Silu).then_inc(s_done, 1)

        take_x(0, 0)
        take_x(0, 1)
        silu(0, 0)

        def step(i, n, ahead):
            act.wait_ge(g_flipped, 2 * i + n + 1)
            wait(act, y_done, 2 * i + n - 1)
            nc.scalar.copy(gT[:, n, :, :], gT_ps[n][:, :, :]).then_inc(gT_out, 1)
            if ahead:
                silu(*((i, 1) if n == 0 else (i + 1, 0)))
            if ahead == 2:
                take_x(i + 1, n)

        tiles(act, step)

    @block.vector
    def _(dve):
        def gated(i, n):
            dve.wait_ge(s_done, 2 * i + n + 1)
            wait(dve, g_flipped, 2 * i + n - 1)
            nc.vector.tensor_tensor(g[:, n, :], s[:, n, :], h2[n][:, :], ALU.mult).then_inc(g_done, 1)

        gated(0, 0)

        def step(i, n, ahead):
            if ahead:
                gated(*((i, 1) if n == 0 else (i + 1, 0)))
            dve.wait_ge(y_done, 2 * i + n + 1)
            wait(dve, stored[n], i * 16)
            nc.vector.tensor_copy(y[:, n, :], y_ps[:, 0, :]).then_inc(y_out, 1)

        tiles(dve, step)

    ctx.close()


def experts1(nc, keep, R, w_in, w_out, w_loaded, rows_out, ident, load_w):
    ctx = ExitStack()

    def sb(name, shape, dt=F32):
        return ctx.enter_context(nc.sbuf_tensor(f"e1_{name}", shape, dt))

    def sem(name):
        return keep.enter_context(nc.semaphore(f"e1_{name}"))

    rows_in = R["rows"]
    tail = CAP - 2 * ROWS
    KH = F1 // 128
    half = 2 * F1
    assert KH * D == half
    parts = sb("parts", [128, 2, 2, 2, half], F32R)
    w_raw = (w_in.rearrange("p n c f -> p n (c f)"), w_out.rearrange("p n k d -> p n (k d)"))
    win_h, win_l = (parts[:, k, :, 0, :].rearrange("p n (c f) -> p n c f", c=2) for k in range(2))
    wout_h, wout_l = (parts[:, k, :, 1, :].rearrange("p n (k d) -> p n k d", d=D) for k in range(2))
    xg = sb("xg", [128, 2, 3, D])
    xT_h, xT_l = sb("xT_h", [128, 2, 2, CAP], F32R), sb("xT_l", [128, 2, 2, CAP], F32R)
    hT_h, hT_l = sb("hT_h", [128, KH, CAP], F32R), sb("hT_l", [128, KH, CAP], F32R)
    yT = sb("yT", [128, 2, CAP])
    y = sb("y", [128, 3, D])

    def pb(name):
        return ctx.enter_context(nc.psum_tensor(f"e1_{name}", [128, 512], F32))

    x_ps, y_ps = ([pb(f"{n}{k}") for k in range(2)] for n in ("x_ps", "y_ps"))
    h_ps = [pb(f"h_ps{k}") for k in range(4)]
    yT_ps = h_ps[2:]
    xg_loaded = [sem(f"xg_loaded{n}") for n in range(2)]
    stored = sem("stored")
    scattered = sem("scattered")
    w_high, win_low, wout_low = sem("w_high"), sem("win_low"), sem("wout_low")
    x_flipped, x_high, xT_out, h_done, h_high, h_out = (
        sem(n) for n in ("x_flipped", "x_high", "xT_out", "h_done", "h_high", "h_out"))
    yT_done, yT_act, yT_dve = (sem(n) for n in ("yT_done", "yT_act", "yT_dve"))
    y_flipped, y_act, y_dve = (sem(n) for n in ("y_flipped", "y_act", "y_dve"))
    in_v = rows_in.rearrange("(e s) d -> e s d", s=CAP)
    out_v = rows_out.rearrange("(e s) d -> e s d", s=CAP)
    ROWT = [(r, min(ROWS, CAP - r * ROWS)) for r in range(3)]
    CHUNKS = 4
    pool_waits = sem("pool_waits")

    def experts(eng, step):
        step(0, 0, 2)
        step(0, 1, 2)
        with eng.Fori(1, E_N // 2 - 1) as i:
            step(i, 0, 2)
            step(i, 1, 2)
        step(E_N // 2 - 1, 0, 1)
        step(E_N // 2 - 1, 1, 0)

    def behind(i, n):
        return (i, 1) if n == 0 else (i + 1, 0)

    def is_first(i, n):
        return isinstance(i, int) and 2 * i + n == 0

    def before(i, n):
        return (i, 0) if n == 1 else (i - 1, 1)

    block = ctx.enter_context(nc.Block())

    @block.sync
    def _(sp):
        def load_x(i, n):
            wait(sp, x_flipped, 2 * i + n - 1)
            src = in_v[2 * i + n]
            sp.dma_start(xg[:, n, 0:2, :], src[0:2 * ROWS, :].rearrange("(r p) d -> p r d", p=ROWS))\
                .then_inc(xg_loaded[n], 16)
            sp.dma_start(xg[0:tail, n, 2, :], src[2 * ROWS:CAP, :]).then_inc(xg_loaded[n], 16)

        sp.wait_ge(scattered, SCATTERED)
        for n in range(2):
            load_x(0, n)

        def step(i, n, ahead):
            if ahead == 2:
                load_x(i + 1, n)
                sp.wait_ge(w_high, CHUNKS * (2 * i + n + 1))
                sp.wait_ge(win_low, 2 * i + n + 1)
                sp.wait_ge(wout_low, 2 * i + n + 1)
                load_w(sp, i + 1, n)

        experts(sp, step)

    @block.gpsimd
    def _(pool):
        def await_(sem_, value):
            if not (isinstance(value, int) and value <= 0):
                pool.wait_ge(sem_, value)
                pool.sem_inc(pool_waits, 1)

        def low_out(i, n):
            await_(w_high, CHUNKS * (2 * i + n) + CHUNKS)
            nc.gpsimd.tensor_tensor(parts[:, 1, n, 1, :], w_raw[1][:, n, :], parts[:, 0, n, 1, :].bitcast(F32),
                                    ALU.subtract).then_inc(wout_low, 1)

        scatter_rows(nc, R, scattered)
        pool.wait_ge(scattered, SCATTERED)
        low_out(0, 0)

        def step(i, n, ahead):
            if ahead:
                low_out(*behind(i, n))
            await_(y_act, 2 * i + n + 1)
            await_(y_dve, 2 * i + n + 1)
            dst = out_v[2 * i + n]
            pool.dma_start(dst[0:2 * ROWS, :].rearrange("(r p) d -> p r d", p=ROWS), y[:, 0:2, :]).then_inc(stored, 16)
            pool.dma_start(dst[2 * ROWS:CAP, :], y[0:tail, 2, :]).then_inc(stored, 16)

        experts(pool, step)
        pool.wait_ge(stored, 32 * E_N)

    @block.tensor
    def _(pe):
        def products(out, terms):
            for n, (a, b) in enumerate(terms):
                last = nc.tensor.matmul(out, a, b, start=(n == 0), stop=(n == len(terms) - 1))
            return last

        def flip_x(i, n):
            pe.wait_ge(xg_loaded[n], 32 * (i + 1))
            wait(pe, xT_out, 2 * i + n)
            for c in range(2):
                for r, k in ROWT:
                    last = nc.tensor.transpose(x_ps[c][:, r * ROWS:r * ROWS + k],
                                               xg[0:k, n, r, c * 128:(c + 1) * 128], ident[0:k, 0:k])
            last.then_inc(x_flipped, 1)

        def flip_y(i, n):
            pe.wait_ge(yT_act, 2 * i + n + 1)
            pe.wait_ge(yT_dve, 2 * i + n + 1)
            wait(pe, y_act, 2 * i + n)
            wait(pe, y_dve, 2 * i + n)
            for r, k in ROWT:
                for m in range(2):
                    last = nc.tensor.transpose(y_ps[r // 2][0:k, (r % 2) * D + m * 128:(r % 2) * D + (m + 1) * 128],
                                               yT[:, m, r * ROWS:r * ROWS + k], ident[:, :])
            last.then_inc(y_flipped, 1)

        flip_x(0, 0)

        def step(i, n, ahead):
            e = 2 * i + n
            pe.wait_ge(win_low, e + 1)
            pe.wait_ge(xT_out, e + 1)
            for m in range(KH):
                wait(pe, h_out, e * KH + m + 1 - 4)
                if m == 2:
                    wait(pe, yT_act, e)
                    wait(pe, yT_dve, e)
                cols = slice(m * 128, (m + 1) * 128)
                products(h_ps[m % 4][:, 0:CAP], [t for c in range(2) for t in (
                    (win_h[:, n, c, cols], xT_h[:, n, c, :]), (win_h[:, n, c, cols], xT_l[:, n, c, :]),
                    (win_l[:, n, c, cols], xT_h[:, n, c, :]))]).then_inc(h_done, 1)
            if not is_first(i, n):
                flip_y(*before(i, n))
            if ahead:
                flip_x(*behind(i, n))
            pe.wait_ge(h_out, (e + 1) * KH)
            pe.wait_ge(wout_low, e + 1)
            for m in range(2):
                cols = slice(m * 128, (m + 1) * 128)
                last = products(yT_ps[m][:, 0:CAP], [t for k in range(KH) for t in (
                    (wout_h[:, n, k, cols], hT_h[:, k, :]), (wout_h[:, n, k, cols], hT_l[:, k, :]),
                    (wout_l[:, n, k, cols], hT_h[:, k, :]))])
            last.then_inc(yT_done, 1)

        experts(pe, step)
        flip_y(E_N // 2 - 1, 1)

    def await_y(eng, i, n):
        eng.wait_ge(y_flipped, 2 * i + n + 1)
        wait(eng, stored, 32 * (2 * i + n))

    @block.scalar
    def _(act):
        def round_w(i, n, part):
            if part == 0:
                act.wait_ge(w_loaded[n], 32 * (i + 1))
                wait(act, yT_done, 2 * i + n - 1)
            cols = slice(part % 2 * F1, (part % 2 + 1) * F1)
            nc.scalar.copy(parts[:, 0, n, part // 2, cols], w_raw[part // 2][:, n, cols]).then_inc(w_high, 1)

        def round_x(i, n):
            act.wait_ge(x_flipped, 2 * i + n + 1)
            wait(act, h_done, (2 * i + n - 1) * KH)
            for c in range(2):
                last = nc.scalar.copy(xT_h[:, n, c, :], x_ps[c][:, 0:CAP])
            last.then_inc(x_high, 1)

        for part in range(CHUNKS):
            round_w(0, 0, part)
        round_x(0, 0)

        def step(i, n, ahead):
            e = 2 * i + n
            for m in range(KH):
                act.wait_ge(h_done, e * KH + m + 1)
                if m == 0:
                    wait(act, yT_done, e)
                nc.scalar.activation(hT_h[:, m, :], h_ps[m % 4][:, 0:CAP], ACT.Relu).then_inc(h_high, 1)
                if ahead and m % 2 == 1:
                    round_w(*behind(i, n), m // 2)
            if not is_first(i, n):
                bi, bn = before(i, n)
                await_y(act, bi, bn)
                nc.scalar.copy(y[:, 0:2, :], y_ps[0][:, :].rearrange("p (r d) -> p r d", d=D)).then_inc(y_act, 1)
            if ahead:
                round_x(*behind(i, n))
            act.wait_ge(yT_done, e + 1)
            wait(act, y_flipped, e)
            nc.scalar.copy(yT[:, 0, :], yT_ps[0][:, 0:CAP]).then_inc(yT_act, 1)

        experts(act, step)
        await_y(act, E_N // 2 - 1, 1)
        nc.scalar.copy(y[:, 0:2, :], y_ps[0][:, :].rearrange("p (r d) -> p r d", d=D)).then_inc(y_act, 1)

    @block.vector
    def _(dve):
        def low_in(i, n):
            dve.wait_ge(w_high, CHUNKS * (2 * i + n) + 2)
            nc.vector.tensor_tensor(parts[:, 1, n, 0, :], w_raw[0][:, n, :], parts[:, 0, n, 0, :].bitcast(F32),
                                    ALU.subtract).then_inc(win_low, 1)

        def low_x(i, n):
            dve.wait_ge(x_high, 2 * i + n + 1)
            for c in range(2):
                last = nc.vector.tensor_tensor(xT_l[:, n, c, :], x_ps[c][:, 0:CAP], xT_h[:, n, c, :].bitcast(F32),
                                               ALU.subtract)
            last.then_inc(xT_out, 1)

        low_in(0, 0)
        low_x(0, 0)

        def step(i, n, ahead):
            e = 2 * i + n
            for m in range(KH):
                dve.wait_ge(h_high, e * KH + m + 1)
                nc.vector.scalar_tensor_tensor(out=hT_l[:, m, :], in0=h_ps[m % 4][:, 0:CAP], scalar=0.0,
                                               in1=hT_h[:, m, :].bitcast(F32), op0=ALU.max,
                                               op1=ALU.subtract).then_inc(h_out, 1)
                if ahead and m == 4:
                    low_in(*behind(i, n))
            if not is_first(i, n):
                bi, bn = before(i, n)
                await_y(dve, bi, bn)
                nc.vector.tensor_copy(y[0:tail, 2, :], y_ps[1][0:tail, 0:D]).then_inc(y_dve, 1)
            if ahead:
                low_x(*behind(i, n))
            dve.wait_ge(yT_done, e + 1)
            wait(dve, y_flipped, e)
            nc.vector.tensor_copy(yT[:, 1, :], yT_ps[1][:, 0:CAP]).then_inc(yT_dve, 1)

        experts(dve, step)
        await_y(dve, E_N // 2 - 1, 1)
        nc.vector.tensor_copy(y[0:tail, 2, :], y_ps[1][0:tail, 0:D]).then_inc(y_dve, 1)

    ctx.close()


def combine(nc, keep, R, x_sb, rows, out):
    ctx = ExitStack()
    T = R["tag"]

    def sem(name):
        return keep.enter_context(nc.semaphore(f"{T}_{name}"))

    K = 2 if out is not None else 3
    RING = 4
    got = ctx.enter_context(nc.sbuf_tensor(f"{T}_got", [128, RING, 3, D], F32))
    gathered = [sem(f"gathered{n}") for n in range(RING)]
    shared_in = [sem(f"shared_in{n}") for n in range(RING)]
    added, stored = sem("added"), sem("x_stored")
    block = ctx.enter_context(nc.Block())

    @block.gpsimd
    def _(pool):
        for b in range(NB):
            if b >= RING:
                pool.wait_ge(added, K * (b - RING + 1))
            for k in range(2):
                nc.gpsimd.indirect_dma_start(
                    out=got[0:NQ, b % RING, k, :], out_offset=None, in_=rows,
                    in_offset=bass.IndirectOffsetOnAxis(ap=R["slot"][0:NQ, k, b:b + 1], axis=0),
                    bounds_check=rows.shape[0] - 1, oob_is_err=False).then_inc(gathered[b % RING], 16)

    @block.sync
    def _(sp):
        if K == 3:
            for b in range(NB):
                if b >= RING:
                    sp.wait_ge(added, K * (b - RING + 1))
                sp.dma_start(got[0:NQ, b % RING, 2, :], rows[b * NQ:(b + 1) * NQ, :]).then_inc(shared_in[b % RING], 16)
        else:
            for b in range(NB):
                sp.wait_ge(added, K * (b + 1))
                sp.dma_start(out[b * NQ:(b + 1) * NQ, :], x_sb[0:NQ, b, :]).then_inc(stored, 16)
            sp.wait_ge(stored, 16 * NB)

    @block.vector
    def _(dve):
        for b in range(NB):
            dve.wait_ge(gathered[b % RING], 16 * 2 * (b // RING + 1))
            if K == 3:
                dve.wait_ge(shared_in[b % RING], 16 * (b // RING + 1))
            for k in range(K):
                w = R["weight"][0:NQ, k, b:b + 1] if k < 2 else R["tg"][0:NQ]
                if k:
                    dve.wait_ge(added, K * b + k)
                nc.vector.scalar_tensor_tensor(out=x_sb[0:NQ, b, :], in0=got[0:NQ, b % RING, k, :], scalar=w,
                                               in1=x_sb[0:NQ, b, :], op0=ALU.mult, op1=ALU.add).then_inc(added, 1)

    ctx.close()


def flamingo(nc, I, out):
    with ExitStack() as keep:
        def sb(name, shape, dt=F32):
            return keep.enter_context(nc.sbuf_tensor(name, shape, dt))

        x_sb = sb("x_sb", [128, NB, D])
        ident = sb("ident", [128, 128])
        g_sb, tg = sb("g_sb", [128, 4]), sb("tg", [128, 4])
        consts = {"earlier": sb("earlier", [128, 128]), "ones": sb("ones", [128, 128]),
                  "before": sb("before", [128, E_N, E_N]), "list_at": sb("list_at", [128, E_N]),
                  "tile_rows": sb("tile_rows", [128, 16]), "tile_no": sb("tile_no", [128, RT_TILES])}
        slots = [sb(f"slot{n}", [128, 2, NB], I32) for n in range(2)]
        weights = [sb(f"weight{n}", [128, 2, NB]) for n in range(2)]
        table = sb("table", [128, RT_TILES], I32)
        scatter_to = sb("scatter_to", [128, 2, NB], I32)
        n_rows0 = (SH_TILES + RT_TILES) * ROWS
        in0 = nc.dram_tensor("rows_in0", (n_rows0, D), F32, kind="Internal").ap()
        out0 = nc.dram_tensor("rows_out0", (n_rows0, D), F32, kind="Internal").ap()
        in1 = nc.dram_tensor("rows_in1", (E_N * CAP, D), F32, kind="Internal").ap()
        out1 = nc.dram_tensor("rows_out1", (E_N * CAP, D), F32, kind="Internal").ap()

        loaded = keep.enter_context(nc.semaphore("loaded"))
        zeroed = keep.enter_context(nc.semaphore("zeroed"))
        cleared = keep.enter_context(nc.semaphore("cleared"))
        w_loaded = keep.enter_context(nc.semaphore("w_loaded"))

        raw_loaded = [[keep.enter_context(nc.semaphore(f"{w}{n}_loaded")) for w in ("wq", "wk", "wv")] for n in range(2)]
        layer0, attention1, layer1 = (keep.enter_context(ExitStack()) for _ in range(3))
        w12 = layer0.enter_context(nc.sbuf_tensor("w12", [128, (E_N + 1) * 4 * F0], F32))
        w3 = layer0.enter_context(nc.sbuf_tensor("w3", [128, (E_N + 1) * 4 * D], F32))
        raw0 = ExitStack()
        raw = [raw0.enter_context(nc.sbuf_tensor("raw0", [128, 3, 2, H * 16], F32))[:, :, :, :]]

        def load_raw(sp, n):
            for k, w in enumerate(("wq", "wk", "wv")):
                sp.dma_start(raw[n][:, k, :, :], I[f"a{n}_{w}"]).then_inc(raw_loaded[n][k], 16)

        with nc.sbuf_tensor("zeros", [128, 7 * D], F32) as zeros, nc.Block() as block:
            @block.sync
            def _(sp):
                load_raw(sp, 0)
                small = [(x_sb[0:NQ], I["x"]), (ident[:, :], I["ident"]), (g_sb[:, :], I["g"]),
                         (consts["earlier"][:, :], I["earlier"]), (consts["before"][:, :, :], I["before"]),
                         (consts["list_at"][:, :], I["list_at"]), (consts["tile_rows"][:, :], I["tile_rows"]),
                         (consts["tile_no"][:, :], I["tile_no"])]
                for dst, src in small:
                    sp.dma_start(dst, src).then_inc(loaded, 16)
                sp.wait_ge(loaded, 16 * len(small))

            @block.gpsimd
            def _(pool):
                nc.gpsimd.memset(zeros[:, :], 0.0).then_inc(zeroed, 1)
                nc.gpsimd.memset(consts["ones"][:, :], 1.0)
                pool.wait_ge(zeroed, 1)
                v0 = in0[TOKENS:, :].rearrange("(p r) d -> p (r d)", p=128)
                for n in range(5):
                    pool.dma_start(v0[:, n * 7 * D:(n + 1) * 7 * D], zeros[:, :]).then_inc(cleared, 16)
                v1 = in1.rearrange("(p r) d -> p (r d)", p=NQ)
                for n in range(4):
                    pool.dma_start(v1[:, n * 5 * D:(n + 1) * 5 * D], zeros[0:NQ, 0:5 * D]).then_inc(cleared, 16)
                pool.wait_ge(cleared, 16 * 9)

            @block.scalar
            def _(act):
                act.wait_ge(loaded, 16 * 8)
                nc.scalar.activation(tg[:, :], g_sb[:, :], ACT.Tanh)

        def route(n, xn):
            return {"xn": xn, "scatter_to": scatter_to, "tag": f"r{n}", "layer": n, "slot": slots[n], "weight": weights[n], "table": table,
                    "rows": (in0, in1)[n], "first": (TOKENS, 0)[n], "tg": tg[:, 2 * n + 1:2 * n + 2]}


        def load_experts(sp, e):
            sp.dma_start(w12[:, e * 4 * F0:(e + 1) * 4 * F0], I["e0_w12"][e]).then_inc(w_loaded, 16)
            sp.dma_start(w3[:, e * 4 * D:(e + 1) * 4 * D], I["e0_w3"][e]).then_inc(w_loaded, 16)

        attention(nc, keep, AttnShape("a0", 16, True), x_sb, ident, tg, 0, raw[0], raw_loaded[0],
                  {k[3:]: v for k, v in I.items() if k.startswith("a0_")} | {"ctx": I["ctx"]}, load_experts)
        raw0.close()
        raw.append(attention1.enter_context(nc.sbuf_tensor("raw1", [128, 3, 2, H * 64], F32, side="right"))[:, :, :, :])
        with nc.sbuf_tensor("xn0", [128, NB, D], F32) as xn:
            R = route(0, xn)
            routing(nc, keep, R, x_sb, ident, consts, {"gw": I["r0_gw"]})
            experts0(nc, keep, R, w12, w3, w_loaded, out0, ident, lambda sp: load_raw(sp, 1))
        combine(nc, keep, R, x_sb, out0, None)
        layer0.close()
        attention(nc, keep, AttnShape("a1", 64, False), x_sb, ident, tg, 2, raw[1], raw_loaded[1],
                  {k[3:]: v for k, v in I.items() if k.startswith("a1_")} | {"ctx": I["ctx"]})
        attention1.close()

        w_in = layer1.enter_context(nc.sbuf_tensor("w_in", [128, 2, 2, F1], F32))
        w_out = layer1.enter_context(nc.sbuf_tensor("w_out", [128, 2, F1 // 128, D], F32))
        w1_loaded = [keep.enter_context(nc.semaphore(f"w1_loaded{n}")) for n in range(2)]
        win_v = I["e1_w_in"].rearrange("e (c p) i -> e p c i", p=128)
        wout_v = I["e1_w_out"].rearrange("e (k p) d -> e p k d", p=128)

        def load_w(sp, i, n):
            sp.dma_start(w_in[:, n, :, :], win_v[2 * i + n]).then_inc(w1_loaded[n], 16)
            sp.dma_start(w_out[:, n, :, :], wout_v[2 * i + n]).then_inc(w1_loaded[n], 16)

        def load_first(sp):
            load_w(sp, 0, 0)
            load_w(sp, 0, 1)

        with nc.sbuf_tensor("xn1", [128, NB, D], F32) as xn:
            R = route(1, xn)
            routing(nc, keep, R, x_sb, ident, consts, {"gw": I["r1_gw"], "gb": I["r1_gb"]}, load_first)
            experts1(nc, keep, R, w_in, w_out, w1_loaded, out1, ident, load_w)
        combine(nc, keep, R, x_sb, out1, out)


def kernel(**inputs):
    import numpy as np
    import concourse.bacc as bacc
    from concourse.bass_utils import run_bass_kernel_spmd

    f = np.float32
    i = {k: np.asarray(v) for k, v in inputs.items()}

    def columns(a, rows=128):
        return a.reshape(-1, rows, a.shape[-1]).transpose(1, 0, 2)

    def context_rows(a):
        o = np.empty((128, 2, a.shape[-1]), f)
        o[:, 0], o[:64, 1], o[64:, 1] = a[:128], a[128:], a[128:]
        return o

    def wide(a):
        return np.broadcast_to(a, (128,) + a.shape)

    ctxT = np.zeros((NB, 128, 2, NKP), f)
    for b in range(NB):
        ctxT[b, :, :, :NK] = context_rows(i["ctx_768"][b].T)
    p = np.arange(128)
    wo0 = np.zeros((4, 32, 4, D), f)
    wo0[:, :16] = i["L0_xattn_Wo"].reshape(4, 4, 16, D).transpose(1, 2, 0, 3)
    w1 = np.concatenate([i["L0_ffn_ew1"], i["L0_ffn_sw1"][None]])
    w2 = np.concatenate([i["L0_ffn_ew2"], i["L0_ffn_sw2"][None]])
    w3 = np.concatenate([i["L0_ffn_ew3"], i["L0_ffn_sw3"][None]])
    w12 = np.stack([w1, w2], 1).reshape(E_N + 1, 2, 2, 128, F0).transpose(0, 3, 1, 2, 4)
    arrays = {
        "x": i["x"].transpose(1, 0, 2), "ctx": ctxT, "ident": np.eye(128, dtype=f),
        "g": wide(np.stack([i["g_xattn"][0], i["g_ffn"][0], i["g_xattn"][1], i["g_ffn"][1]])),
        "earlier": (p[:, None] < p[None, :]).astype(f),
        "before": wide((np.arange(E_N)[None, :] < np.arange(E_N)[:, None]).astype(f)),
        "list_at": wide((np.arange(E_N) * CAP).astype(f)),
        "tile_rows": wide((np.arange(16) * ROWS).astype(f)), "tile_no": wide(np.arange(RT_TILES).astype(f)),
        "a0_wq": columns(i["L0_xattn_Wq"]), "a0_wk": context_rows(i["L0_xattn_Wk"]),
        "a0_wv": context_rows(i["L0_xattn_Wv"]), "a0_wo": wo0.reshape(128, 4, D),
        "a0_bq": i["L0_xattn_bq"].reshape(2, 128).T, "a0_bk": i["L0_xattn_bk"].reshape(2, 128).T,
        "a0_bv": wide(i["L0_xattn_bv"]), "a0_bo": wide(i["L0_xattn_bo"]),
        "a0_head_mask": (p[:, None] // 16 == np.arange(8)[None, :]).astype(f),
        "r0_gw": columns(i["L0_ffn_gate_w"]), "e0_w12": w12.reshape(E_N + 1, 128, 4 * F0),
        "e0_w3": w3.reshape(E_N + 1, 4, 128, D).transpose(0, 2, 1, 3).reshape(E_N + 1, 128, 4 * D),
        "a1_wq": columns(i["L1_xattn_w_q"]), "a1_wk": context_rows(i["L1_xattn_w_k"]),
        "a1_wv": context_rows(i["L1_xattn_w_v"]), "a1_wo": columns(i["L1_xattn_w_o"]),
        "a1_bo": wide(i["L1_xattn_b_o"]),
        "r1_gw": columns(i["L1_ffn_W_router"].T), "r1_gb": wide(i["L1_ffn_b_router"]),
        "e1_w_in": i["L1_ffn_experts_inter"], "e1_w_out": i["L1_ffn_experts_out"],
    }
    arrays = {f"in_{k}": np.ascontiguousarray(v) for k, v in arrays.items()}
    nc = bacc.Bacc("TRN2", target_bir_lowering=False, num_devices=1)
    aps = {k[3:]: nc.dram_tensor(k, v.shape, mybir.dt.from_np(v.dtype), kind="ExternalInput").ap()
           for k, v in arrays.items()}
    out = nc.dram_tensor("out_x", (TOKENS, D), F32, kind="ExternalOutput").ap()
    flamingo(nc, aps, out)
    got = run_bass_kernel_spmd(nc, [arrays], core_ids=[0]).results[0]["out_x"]
    return got.reshape(NB, NQ, D)
```

```python
from contextlib import ExitStack

import concourse.bass as bass
from concourse import mybir

F32 = mybir.dt.float32
F32R = mybir.dt.float32r
I32 = mybir.dt.int32
ALU = mybir.AluOpType
ACT = mybir.ActivationFunctionType
AX = mybir.AxisListType

NB = 16
NQ = 112
D = 256
CD = 192
NK = 375
NKP = NK + 1
KC = 125
NC = NK // KC
H = 16
EPS = 1e-5
S_AHEAD, MAX_AHEAD, EXP_AHEAD = 3, 3, 2
HALF = (slice(0, 64), slice(64, 128))
S_BANK = (0, 1, 2) * 4 + (0, 1, 0, 2)
S_BACK = [next(n for n in range(1, H + 1) if S_BANK[(h - n) % H] == S_BANK[h]) for h in range(H)]
T_BANKS = 2
P_RING = 4
PT_RING = 8
O_BLOCKS = 4


class AttnShape:

    def __init__(self, tag, dh, bias):
        self.tag, self.dh, self.bias = tag, dh, bias
        self.inner = H * dh
        self.mt = self.inner // 128
        self.hpt = H // self.mt
        self.scale = float(dh) ** -0.5
        self.hph = self.hpt // 2
        self.group = 4 if dh == 16 else 2
        self.vw = 128 // self.group
        self.ngroups = H // self.group
        self.turn = 5
        self.late_norm = dh == 16
        self.project_at = 3
        self.nout = self.ngroups // O_BLOCKS
        self.mq = self.mt // 2
        self.vparts = 1 if dh == 16 else 2
        self.vwide = self.inner // self.vparts
        self.vheads = H // self.vparts
        self.p_banks = 1 if dh == 16 else 2
        v = [[("v", part, c) for c in range(NC)] for part in range(self.vparts)]
        if dh == 16:
            at = {6: [("x", 0)], 7: [("x", 1)], 8: [("q", 0)], 10: [("k", 0)], 12: [("k", 1)], 15: [("q", 1)],
                  17: [v[0][0]], 19: [v[0][1]], 20: [v[0][2]]}
            self.split_at = 5
        else:
            at = {7: [("x", 0), ("x", 1)], 8: [("n", 0)], 9: [("q", 0), ("k", 0)], 10: [("n", 1), ("k", 1)],
                  11: [v[0][0]], 12: [("k", 2)], 13: [("q", 1)], 14: [v[0][1]], 16: [v[0][2], ("k", 3), ("k", 4)],
                  17: [("k", 5)], 18: [v[1][0]], 19: [v[1][1]], 20: [("k", 7), ("k", 6)], 21: [v[1][2]]}
            self.split_at = 6
        self.next_at, self.this_at = self.split_steps(at)
        self.next_out, self.this_out = self.split_steps({s + 1: ps for s, ps in at.items()})
        self.order = [p for s in sorted(at) for p in at[s]]
        self.before = [p for s in sorted(self.next_at) for p in self.next_at[s]]
        self.before_out = [p for s in sorted(self.next_out) for p in self.next_out[s]]
        self.behind_y = next(p for s in sorted(at) if s > H + self.project_at for p in at[s])
        self.np = len(self.order)
        assert self.np % self.p_banks == 0
        self.scalar_only = "n" if dh == 16 else "nv"
        self.early = [p for p in self.order if p[0] in self.scalar_only or p[0] != "v"]
        self.late = [p for p in self.order if p[0] not in self.scalar_only]
        self.last_v = [("v", part, NC - 1) for part in range(self.vparts)]

    @staticmethod
    def split_steps(at):
        assert max(at) - H < min(at)
        return {s: ps for s, ps in at.items() if s < H}, {s - H: ps for s, ps in at.items() if s >= H}

    def piece(self, p):
        return self.order.index(p)

    def scores_need(self, h):
        return max(("k", h // self.hpt), ("q", h // (H // 2)), key=self.piece)

    def high(self, t, p):
        return t * len(self.early) + self.early.index(p) + 1

    def out(self, t, p):
        return t * len(self.late) + self.late.index(p) + 1

    def pv_step(self, g):
        return self.group * g + self.group + 1


def walk(eng, turn, step):
    for h in range(turn):
        step(0, h, False, True)
    with eng.Fori(0, NB - 1) as i:
        for h in range(turn, H):
            step(i, h, True, True)
        for h in range(turn):
            step(i + 1, h, True, True)
    for h in range(turn, H):
        step(NB - 1, h, True, False)


def wait(eng, sem, value):
    if not (isinstance(value, int) and value <= 0):
        eng.wait_ge(sem, value)


def attention(nc, keep, A, x_sb, ident, tg, tg_col, raw, raw_loaded, dram, load_experts=None, first=None):
    T = A.tag
    ctx = ExitStack()

    def sb(name, shape, dt=F32):
        return ctx.enter_context(nc.sbuf_tensor(f"{T}_{name}", shape, dt))

    def sem(name):
        return keep.enter_context(nc.semaphore(f"{T}_{name}"))

    wq_h, wq_l = sb("wq_h", [128, 2, A.inner], F32R), sb("wq_l", [128, 2, A.inner], F32R)
    wk_h, wk_l = sb("wk_h", [128, 2, A.inner], F32R), sb("wk_l", [128, 2, A.inner], F32R)
    wv_h, wv_l = sb("wv_h", [128, 2, A.inner], F32R), sb("wv_l", [128, 2, A.inner], F32R)
    wo = sb("wo", [128, A.ngroups, D])
    bo = sb("bo", [128, D])
    k_both = sb("k_both", [128, A.mt, 2, NKP], F32R)
    q_twice = sb("q_twice", [128, A.mt, 2, A.hph, NQ], F32R)
    qT_l = sb("qT_l", [128, A.mt, A.hph, NQ], F32R)
    if not A.bias:
        q_rows = sb("q_rows", [128, A.inner])
    v_sb = sb("v_sb", [128, NC, H, A.vw])
    ctx_raw = sb("ctx_raw", [128, 2, NKP])
    ctx_h, ctx_l = sb("ctx_h", [128, NKP], F32R), sb("ctx_l", [128, NKP], F32R)
    ctx_b = sb("ctx_b", [128, NKP], F32R)
    xn = sb("xn", [128, D])
    xT_h, xT_l = sb("xT_h", [128, 2, NQ], F32R), sb("xT_l", [128, 2, NQ], F32R)
    probs, pT = sb("probs", [128, P_RING, NKP]), sb("pT", [128, PT_RING, NC * NQ])
    if A.bias:
        oT = sb("oT", [128, A.ngroups, NQ])
    else:
        oT_h, oT_l = sb("oT_h", [128, A.ngroups, NQ], F32R), sb("oT_l", [128, A.ngroups, NQ], F32R)
        wo_h, wo_l = sb("wo_h", [128, A.ngroups, D], F32R), sb("wo_l", [128, A.ngroups, D], F32R)
    if not A.bias:
        y_sb = sb("y_sb", [128, D])
    nmax, rsum, rinv = sb("nmax", [128, H]), sb("rsum", [128, H]), sb("rinv", [128, H])
    stats, mv = sb("stats", [128, NB, 6]), sb("mv", [128, NB, 2])
    var, rstd, tmp = sb("var", [128, NB]), sb("rstd", [128, NB]), sb("tmp", [128, NB])
    if A.bias:
        bq, bk, bv = sb("bq", [128, A.mt]), sb("bk", [128, A.mt]), sb("bv", [128, A.inner])
        head_mask = sb("head_mask", [128, A.hph, 1])
        q_h = sb("q_h", [128, 2, NQ], F32R)
        q_l = sb("q_l", [128, NQ], F32R)
        spare = raw.rearrange("p k c n -> p k (c n)")
        inv_wide = spare[:, 0, 0:H * A.vw].rearrange("p (h w) -> p h w", h=H)
        o_inv = spare[:, 1, 0:O_BLOCKS * NQ]
        q_t = spare[:, 2, 0:NQ]
        y_sb = spare[:, 2, D:2 * D]

    def pb(name):
        return ctx.enter_context(nc.psum_tensor(f"{T}_{name}", [128, 512], F32))

    s_ps = [pb(f"s_ps{n}") for n in range(max(S_BANK) + 1)]
    t_ps = [pb(f"t_ps{n}") for n in range(T_BANKS)]
    o_ps = pb("o_ps")
    p_ps = [pb(f"p_ps{n}") for n in range(A.p_banks)]
    y_ps = pb("y_ps") if A.bias else p_ps[A.piece(A.behind_y) % A.p_banks]

    small_loaded = sem("small_loaded")
    ctx_loaded = sem("ctx_loaded")
    w_high = sem("w_high")
    w_split = sem("w_split")
    stats_done = sem("stats_done")
    dve_self = sem("dve_self")
    pool_waits = sem("pool_waits")
    std_done = sem("std_done")
    v_filled = sem("v_filled") if A.bias else None
    ctx_high = sem("ctx_high")
    ctx_split = sem("ctx_split")
    xn_done = sem("xn_done")
    piece_done = sem("piece_done")
    piece_high = sem("piece_high")
    piece_out = sem("piece_out")
    q_biased = sem("q_biased") if A.bias else None
    q_masked = sem("q_masked")
    scores = sem("scores")
    max_done = sem("max_done")
    exp_done = sem("exp_done")
    inv_done = sem("inv_done")
    normed = None if A.late_norm else sem("normed")
    flipped = sem("flipped")
    pT_done = sem("pT_done")
    pv_done = sem("pv_done")
    o_high = None if A.late_norm else sem("o_high")
    o_out = sem("o_out")
    sums_done = sem("sums_done") if A.bias else None
    sums_out = sem("sums_out") if A.bias else None
    proj_done = sem("proj_done")
    x_updated = sem("x_updated")

    n_small = 2 + (4 if A.bias else 0)
    SPLIT = [(raw[:, n, :, :], high[:, :, :], low[:, :, :], raw_loaded[n], 16)
             for n, (high, low) in enumerate(((wq_h, wq_l), (wk_h, wk_l), (wv_h, wv_l)))]
    if not A.bias:
        SPLIT.append((wo[:, :, :], wo_h[:, :, :], wo_l[:, :, :], small_loaded, 16 * n_small))

    if first is not None:
        combined = first(v_sb[:, :, :, :].rearrange("p c h w -> p (c h w)"))
    block = ctx.enter_context(nc.Block())

    @block.sync
    def _(sp):
        sp.dma_start(ctx_raw[:, :, :], dram["ctx"][0]).then_inc(ctx_loaded, 16)
        sp.dma_start(bo[:, :], dram["bo"]).then_inc(small_loaded, 16)
        sp.dma_start(wo[:, :, :], dram["wo"]).then_inc(small_loaded, 16)
        if A.bias:
            sp.dma_start(bq[:, :], dram["bq"]).then_inc(small_loaded, 16)
            sp.dma_start(bk[:, :], dram["bk"]).then_inc(small_loaded, 16)
            sp.dma_start(bv[:, :], dram["bv"]).then_inc(small_loaded, 16)
            sp.dma_start(head_mask[:, :, 0], dram["head_mask"]).then_inc(small_loaded, 16)
        if first is not None:
            combined.sync(sp)
        start = 1
        if load_experts is not None:
            for b in range(1, E_N + 2):
                sp.wait_ge(ctx_split, b)
                sp.dma_start(ctx_raw[:, :, :], dram["ctx"][b]).then_inc(ctx_loaded, 16)
                load_experts(sp, b - 1)
            start = E_N + 2
        with sp.Fori(start, NB) as b:
            sp.wait_ge(ctx_split, b)
            sp.dma_start(ctx_raw[:, :, :], dram["ctx"][b]).then_inc(ctx_loaded, 16)

    @block.gpsimd
    def _(pool):
        def await_(sem_, value):
            if not (isinstance(value, int) and value <= 0):
                pool.wait_ge(sem_, value)
                pool.sem_inc(pool_waits, 1)

        def split_context(b):
            await_(ctx_loaded, b * 16 + 16)
            await_(piece_done, b * A.np)
            nc.gpsimd.tensor_copy(ctx_h[:, :], ctx_raw[:, 0, :])
            nc.gpsimd.tensor_copy(ctx_b[:, :], ctx_raw[:, 1, :]).then_inc(ctx_high, 1)
            pool.wait_ge(ctx_high, b * 2 + 1)
            nc.gpsimd.tensor_tensor(ctx_l[:, :], ctx_raw[:, 0, :], ctx_h[:, :].bitcast(F32), ALU.subtract)\
                .then_inc(ctx_high, 1)
            pool.wait_ge(ctx_high, b * 2 + 2)
            nc.gpsimd.tensor_tensor(ctx_b[64:128, :], ctx_raw[64:128, 1, :], ctx_b[64:128, :].bitcast(F32),
                                    ALU.subtract).then_inc(ctx_split, 1)
            await_(ctx_split, b + 1)

        if A.vw > A.dh:
            nc.gpsimd.memset(v_sb[:, :, :, :], 1.0).then_inc(v_filled, 1)
        if first is not None:
            combined.pool(pool)
        split_context(0)

        def mask_q(t, m):
            await_(piece_out, A.out(t, ("q", m)))
            for part, masked in ((q_h[:, 0, :], q_twice[:, m, 0, :, :]), (q_h[:, 1, :], q_twice[:, m, 1, :, :]),
                                 (q_l[:, :], qT_l[:, m, :, :])):
                last = nc.gpsimd.tensor_tensor(
                    masked, part[:, None, :].bitcast(F32).to_broadcast([128, A.hph, NQ]),
                    head_mask[:, :, :].to_broadcast([128, A.hph, NQ]), ALU.mult)
            last.then_inc(q_masked, 1)

        def double_q(t, m):
            await_(piece_out, A.out(t, ("q", m)))
            ms = slice(m * A.mq, (m + 1) * A.mq)
            for odd, mine in enumerate(HALF):
                other = HALF[1 - odd]
                nc.gpsimd.tensor_copy(q_twice[other, ms, odd, 0, :], q_twice[mine, ms, odd, 0, :]).then_inc(q_masked, 1)
                await_(q_masked, 4 * t + 2 * m + odd + 1)

        prepare_q = mask_q if A.bias else double_q
        for m in range(2):
            prepare_q(0, m)

        def step(b, h, prev, nxt):
            if h == A.split_at and nxt:
                split_context(b + 1)
            if nxt:
                for p in A.next_at.get(h, []):
                    if p[0] == "q":
                        prepare_q(b + 1, p[1])

        walk(pool, A.turn, step)

    @block.scalar
    def _(act):
        def root():
            act.wait_ge(stats_done, 1)
            nc.scalar.activation(rstd[0:NQ, :], var[0:NQ, :], ACT.Sqrt).then_inc(std_done, 1)

        if first is None:
            root()
        for whole, high, _, loaded, count in SPLIT:
            act.wait_ge(loaded, count)
            nc.scalar.copy(high, whole).then_inc(w_high, 1)
        if first is not None:
            root()
        if A.bias:
            act.wait_ge(small_loaded, 16 * n_small)

        def piece_scalar(t, p):
            k = A.piece(p)
            src = p_ps[k % A.p_banks]
            if p[0] == "q" and A.bias:
                act.wait_ge(q_biased, t * 2 + p[1] + 1)
                wait(act, q_masked, t * 2 + p[1])
                for odd, mine in enumerate(HALF):
                    for rows in HALF:
                        last = nc.scalar.copy(q_h[rows, odd, :], q_t[mine, :])
                last.then_inc(piece_high, 1)
                return
            act.wait_ge(piece_done, t * A.np + k + 1)
            if p[0] == "x":
                nc.scalar.activation(xT_h[:, p[1], :], src[:, 0:NQ], ACT.Copy).then_inc(piece_high, 1)
            elif p[0] == "v":
                nc.scalar.activation(v_sb[0:KC, p[2], p[1] * A.vheads:(p[1] + 1) * A.vheads, 0:A.dh],
                                     src[0:KC, 0:A.vwide].rearrange("p (h d) -> p h d", d=A.dh), ACT.Copy)\
                    .then_inc(piece_high, 1)
            elif p[0] == "n":
                nc.scalar.activation(q_rows[0:NQ, p[1] * 512:(p[1] + 1) * 512], src[0:NQ, :], ACT.Copy,
                                     scale=A.scale).then_inc(piece_high, 1)
            elif p[0] == "q":
                ms = slice(p[1] * A.mq, (p[1] + 1) * A.mq)
                for odd, rows in enumerate(HALF):
                    last = nc.scalar.activation(q_twice[rows, ms, odd, 0, :],
                                                src[rows, 0:A.mq * NQ].rearrange("p (m q) -> p m q", q=NQ), ACT.Copy)
                last.then_inc(piece_high, 1)
            elif p[0] == "k":
                for odd, rows in enumerate(HALF):
                    if A.bias:
                        last = nc.scalar.activation(k_both[rows, p[1], odd, :], src[rows, 0:NKP], ACT.Identity,
                                                    bias=bk[rows, p[1]:p[1] + 1])
                    else:
                        last = nc.scalar.activation(k_both[rows, p[1], odd, :], src[rows, 0:NKP], ACT.Copy)
                last.then_inc(piece_high, 1)

        def exponent(b, h):
            act.wait_ge(max_done, b * H + h + 1)
            wait(act, flipped, b * H + h + 1 - P_RING)
            nc.scalar.activation(probs[0:NQ, h % P_RING, 0:NK], s_ps[S_BANK[h]][0:NQ, 0:NK], ACT.Exp,
                                 bias=nmax[0:NQ, h:h + 1], accum_out=rsum[0:NQ, h:h + 1]).then_inc(exp_done, 1)

        def take_flipped(b, h):
            act.wait_ge(flipped, b * H + h + 1)
            nc.scalar.copy(pT[0:KC, h % PT_RING, :], t_ps[h % T_BANKS][0:KC, 0:NC * NQ]).then_inc(pT_done, 1)

        def round_output(b, half):
            act.wait_ge(pv_done, b * A.ngroups + O_BLOCKS * (half + 1))
            nc.scalar.copy(oT_h[:, half * O_BLOCKS:(half + 1) * O_BLOCKS, :],
                           o_ps[:, 0:O_BLOCKS * NQ].rearrange("p (g q) -> p g q", q=NQ)).then_inc(o_high, 1)

        def take_sums(b):
            act.wait_ge(sums_done, b + 1)
            nc.scalar.copy(o_inv[:, :], y_ps[:, 0:O_BLOCKS * NQ]).then_inc(sums_out, 1)

        for p in A.before_out:
            if p in A.early:
                piece_scalar(0, p)
        for h in range(EXP_AHEAD):
            exponent(0, h)

        def step(b, h, prev, nxt):
            if not A.late_norm:
                if h == 2 and prev:
                    round_output(b - 1, 1)
                if h == A.pv_step(O_BLOCKS - 1) + 1:
                    round_output(b, 0)
            for p in A.this_out.get(h, []):
                if p in A.early:
                    piece_scalar(b, p)
            if nxt:
                for p in A.next_out.get(h, []):
                    if p in A.early:
                        piece_scalar(b + 1, p)
            if h + EXP_AHEAD < H:
                exponent(b, h + EXP_AHEAD)
            elif nxt:
                exponent(b + 1, h + EXP_AHEAD - H)
            take_flipped(b, h)
            if A.late_norm and h == 0 and prev:
                take_sums(b - 1)

        walk(act, A.turn, step)
        if not A.late_norm:
            round_output(NB - 1, 1)
        if A.late_norm:
            take_sums(NB - 1)

    @block.vector
    def _(dve):
        mine = [0]

        def link(ins):
            mine[0] += 1
            ins.then_inc(dve_self, 1)
            dve.wait_ge(dve_self, mine[0])

        def low(n):
            dve.wait_ge(w_high, n + 1)
            whole, high, low_part, _, _ = SPLIT[n]
            nc.vector.tensor_tensor(low_part, whole, high.bitcast(F32), ALU.subtract).then_inc(w_split, 1)

        def invert():
            dve.wait_ge(std_done, 1)
            link(nc.vector.reciprocal(tmp[0:NQ, :], rstd[0:NQ, :]))
            link(nc.vector.tensor_tensor(rstd[0:NQ, :], tmp[0:NQ, :], tmp[0:NQ, :], ALU.mult))
            link(nc.vector.tensor_tensor(var[0:NQ, :], rstd[0:NQ, :], var[0:NQ, :], ALU.mult))
            link(nc.vector.tensor_scalar(var[0:NQ, :], var[0:NQ, :], -0.5, 1.5, ALU.mult, ALU.add))
            link(nc.vector.tensor_tensor(rstd[0:NQ, :], tmp[0:NQ, :], var[0:NQ, :], ALU.mult))

        def batch_stats(b):
            return nc.vector.bn_stats(stats[0:NQ, b, :], x_sb[0:NQ, b, :])

        if first is not None:
            def between(b):
                last = batch_stats(b)
                if b in (2, 5, 8, 11):
                    low((b - 2) // 3)
                return last

            last = combined.vector(dve, between)
        else:
            for b in range(NB):
                last = batch_stats(b)
        link(last)
        for b in range(NB):
            last = nc.vector.bn_aggr(mv[0:NQ, b, :], stats[0:NQ, b, :])
        link(last)
        nc.vector.tensor_scalar(var[0:NQ, :], mv[0:NQ, :, 1], EPS, None, ALU.add).then_inc(stats_done, 1)
        if first is None:
            low(0)
        invert()
        if first is None:
            for n in range(1, len(SPLIT)):
                low(n)
        dve.wait_ge(small_loaded, 16 * n_small)
        if A.vw > A.dh:
            dve.wait_ge(v_filled, 1)

        def layernorm(b):
            if not isinstance(b, int) or b > 0:
                dve.wait_ge(piece_done, (b - 1) * A.np + A.piece(("x", 1)) + 1)
            nc.vector.tensor_scalar(xn[0:NQ, :], x_sb[0:NQ, bass.ds(b, 1), :].rearrange("p o d -> p (o d)"),
                                    mv[0:NQ, bass.ds(b, 1), 0], rstd[0:NQ, bass.ds(b, 1)],
                                    ALU.subtract, ALU.mult).then_inc(xn_done, 1)

        def piece_vector(t, p):
            if p not in A.late:
                return
            k = A.piece(p)
            src = p_ps[k % A.p_banks]
            if p[0] == "v":
                dve.wait_ge(piece_done, t * A.np + k + 1)
                out = v_sb[0:KC, p[2], p[1] * A.vheads:(p[1] + 1) * A.vheads, 0:A.dh]
                ins = src[0:KC, 0:A.vwide].rearrange("p (h d) -> p h d", d=A.dh)
                nc.vector.tensor_tensor(out, ins, bv[0:KC, :].rearrange("p (h d) -> p h d", d=A.dh),
                                        ALU.add).then_inc(piece_out, 1)
                return
            if p[0] == "q" and A.bias:
                m = p[1]
                dve.wait_ge(piece_done, t * A.np + k + 1)
                nc.vector.tensor_scalar(q_t[:, :], src[:, 0:NQ], bq[:, m:m + 1], A.scale, ALU.add, ALU.mult)\
                    .then_inc(q_biased, 1)
                dve.wait_ge(q_biased, t * 2 + m + 1)
                dve.wait_ge(piece_high, A.high(t, p))
                wait(dve, q_masked, t * 2 + m)
                for odd, rows in enumerate(HALF):
                    last = nc.vector.tensor_tensor(q_l[rows, :], q_t[rows, :], q_h[rows, odd, :].bitcast(F32),
                                                   ALU.subtract)
                last.then_inc(piece_out, 1)
                return
            dve.wait_ge(piece_high, A.high(t, p))
            if p[0] == "x":
                nc.vector.tensor_tensor(xT_l[:, p[1], :], src[:, 0:NQ], xT_h[:, p[1], :].bitcast(F32),
                                        ALU.subtract).then_inc(piece_out, 1)
            elif p[0] == "q":
                ms = slice(p[1] * A.mq, (p[1] + 1) * A.mq)
                for odd, rows in enumerate(HALF):
                    last = nc.vector.tensor_tensor(
                        qT_l[rows, ms, 0, :], src[rows, 0:A.mq * NQ].rearrange("p (m q) -> p m q", q=NQ),
                        q_twice[rows, ms, odd, 0, :].bitcast(F32), ALU.subtract)
                last.then_inc(piece_out, 1)
            else:
                for odd, rows in enumerate(HALF):
                    high, low = k_both[rows, p[1], odd, :].bitcast(F32), k_both[HALF[1 - odd], p[1], odd, :]
                    if A.bias:
                        last = nc.vector.scalar_tensor_tensor(
                            out=low, in0=src[rows, 0:NKP], scalar=bk[rows, p[1]:p[1] + 1], in1=high,
                            op0=ALU.add, op1=ALU.subtract)
                    else:
                        last = nc.vector.tensor_tensor(low, src[rows, 0:NKP], high, ALU.subtract)
                last.then_inc(piece_out, 1)

        def row_max(b, h):
            dve.wait_ge(scores, b * H + h + 1)
            nc.vector.tensor_reduce(nmax[0:NQ, h:h + 1], s_ps[S_BANK[h]][0:NQ, 0:NK], AX.X, ALU.max, negate=True)\
                .then_inc(max_done, 1)

        def normalise(b, h):
            if A.late_norm:
                return
            dve.wait_ge(exp_done, b * H + h + 1)
            nc.vector.reciprocal(rinv[0:NQ, h:h + 1], rsum[0:NQ, h:h + 1]).then_inc(inv_done, 1)
            dve.wait_ge(inv_done, b * H + h + 1)
            p = probs[0:NQ, h % P_RING, 0:NK]
            nc.vector.tensor_scalar(p, p, rinv[0:NQ, h:h + 1], None, ALU.mult).then_inc(normed, 1)

        def invert_sums(b, g):
            dve.wait_ge(exp_done, b * H + (g + 1) * A.group)
            if g == 0:
                wait(dve, sums_done, b)
            heads = slice(g * A.group, (g + 1) * A.group)
            nc.vector.reciprocal(rinv[0:NQ, heads], rsum[0:NQ, heads]).then_inc(inv_done, 1)
            dve.wait_ge(inv_done, 2 * (b * A.ngroups + g) + 1)
            nc.vector.tensor_copy(inv_wide[0:NQ, heads, :], rinv[0:NQ, heads, None].to_broadcast([NQ, A.group, A.vw]))\
                .then_inc(inv_done, 1)

        def take_output(b, half):
            dve.wait_ge(pv_done, b * A.ngroups + O_BLOCKS * (half + 1))
            groups = slice(half * O_BLOCKS, (half + 1) * O_BLOCKS)
            ins = o_ps[:, 0:O_BLOCKS * NQ].rearrange("p (g q) -> p g q", q=NQ)
            if A.late_norm:
                dve.wait_ge(sums_out, b + 1)
                nc.vector.tensor_tensor(oT[:, groups, :], ins, o_inv[:, :].rearrange("p (g q) -> p g q", q=NQ),
                                        ALU.mult).then_inc(o_out, 1)
            else:
                dve.wait_ge(o_high, b * A.nout + half + 1)
                nc.vector.tensor_tensor(oT_l[:, groups, :], ins, oT_h[:, groups, :].bitcast(F32), ALU.subtract)\
                    .then_inc(o_out, 1)

        def update_x(b):
            dve.wait_ge(proj_done, b + 1)
            nc.vector.tensor_tensor(y_sb[0:NQ, :], y_ps[0:NQ, 0:D], bo[0:NQ, :], ALU.add).then_inc(x_updated, 1)
            dve.wait_ge(x_updated, 2 * b + 1)
            xb = x_sb[0:NQ, bass.ds(b, 1), :].rearrange("p o d -> p (o d)")
            nc.vector.scalar_tensor_tensor(out=xb, in0=y_sb[0:NQ, :], scalar=tg[0:NQ, tg_col:tg_col + 1],
                                           in1=xb, op0=ALU.mult, op1=ALU.add).then_inc(x_updated, 1)

        layernorm(0)
        for p in A.before_out:
            piece_vector(0, p)
        for h in range(MAX_AHEAD):
            row_max(0, h)
        normalise(0, 0)

        def step(b, h, prev, nxt):
            if h == 5 and nxt:
                layernorm(b + 1)
            if h + 1 < H:
                normalise(b, h + 1)
            elif nxt:
                normalise(b + 1, 0)
            if h == 2 and prev:
                take_output(b - 1, A.nout - 1)
            if A.nout == 2 and h == A.pv_step(O_BLOCKS - 1) + 1:
                take_output(b, 0)
            for p in A.this_out.get(h, []):
                piece_vector(b, p)
            if nxt:
                for p in A.next_out.get(h, []):
                    piece_vector(b + 1, p)
            if h == A.project_at + 1 and prev:
                update_x(b - 1)
            if h + S_AHEAD < H:
                row_max(b, h + S_AHEAD)
            elif nxt:
                row_max(b + 1, h + S_AHEAD - H)
            if A.late_norm and h % A.group == A.group - 1:
                invert_sums(b, h // A.group)

        walk(dve, A.turn, step)
        take_output(NB - 1, A.nout - 1)
        update_x(NB - 1)

    @block.tensor
    def _(pe):
        def products(out, terms):
            for n, (a, b) in enumerate(terms):
                last = nc.tensor.matmul(out, a, b, start=(n == 0), stop=(n == len(terms) - 1))
            return last

        def await_taken(t, p):
            if p in A.late:
                pe.wait_ge(piece_out, A.out(t, p))
            else:
                pe.wait_ge(piece_high, A.high(t, p))

        def piece_tensor(t, p):
            k = A.piece(p)
            dst = p_ps[k % A.p_banks]
            before = A.order[k - A.p_banks]
            t_before = t - 1 if k < A.p_banks else t
            if not (isinstance(t_before, int) and t_before < 0):
                await_taken(t_before, before)
            if not A.bias and p == A.behind_y:
                wait(pe, x_updated, 2 * t - 1)
            if p[0] == "x":
                pe.wait_ge(xn_done, t + 1)
                nc.tensor.transpose(dst[:, 0:NQ], xn[0:NQ, p[1] * 128:(p[1] + 1) * 128],
                                    ident[0:NQ, 0:NQ]).then_inc(piece_done, 1)
            elif p[0] == "n":
                pe.wait_ge(piece_out, A.out(t, ("x", 1)))
                cols = slice(p[1] * 512, (p[1] + 1) * 512)
                products(dst[0:NQ, :], [
                    t_ for c in range(2) for t_ in (
                        (xT_h[:, c, :], wq_h[:, c, cols]), (xT_h[:, c, :], wq_l[:, c, cols]),
                        (xT_l[:, c, :], wq_h[:, c, cols]))]).then_inc(piece_done, 1)
            elif p[0] == "q" and not A.bias:
                pe.wait_ge(piece_high, A.high(t, ("n", p[1])))
                for n in range(A.mq):
                    cols = slice((p[1] * A.mq + n) * 128, (p[1] * A.mq + n + 1) * 128)
                    last = nc.tensor.transpose(dst[:, n * NQ:(n + 1) * NQ], q_rows[0:NQ, cols], ident[0:NQ, 0:NQ])
                last.then_inc(piece_done, 1)
            elif p[0] == "q":
                pe.wait_ge(piece_out, A.out(t, ("x", 1)))
                for n in range(A.mq):
                    cols = slice((p[1] * A.mq + n) * 128, (p[1] * A.mq + n + 1) * 128)
                    last = products(dst[:, n * NQ:(n + 1) * NQ], [
                        t_ for c in range(2) for t_ in (
                            (wq_h[:, c, cols], xT_h[:, c, :]), (wq_h[:, c, cols], xT_l[:, c, :]),
                            (wq_l[:, c, cols], xT_h[:, c, :]))])
                last.then_inc(piece_done, 1)
            elif p[0] == "k":
                pe.wait_ge(ctx_split, t + 1)
                cols = slice(p[1] * 128, (p[1] + 1) * 128)
                products(dst[:, 0:NKP], [
                    (wk_h[:, 0, cols], ctx_h[:, :]), (wk_h[:, 0, cols], ctx_l[:, :]),
                    (wk_l[:, 0, cols], ctx_h[:, :]),
                    (wk_h[:, 1, cols], ctx_b[:, :]),
                    (wk_l[0:64, 1, cols], ctx_b[0:64, :])]).then_inc(piece_done, 1)
            else:
                pe.wait_ge(ctx_split, t + 1)
                cols = slice(p[1] * A.vwide, (p[1] + 1) * A.vwide)
                keys = slice(p[2] * KC, (p[2] + 1) * KC)
                products(dst[0:KC, 0:A.vwide], [
                    (ctx_h[:, keys], wv_h[:, 0, cols]), (ctx_h[:, keys], wv_l[:, 0, cols]),
                    (ctx_l[:, keys], wv_h[:, 0, cols]),
                    (ctx_b[:, keys], wv_h[:, 1, cols]),
                    (ctx_b[0:64, keys], wv_l[0:64, 1, cols])]).then_inc(piece_done, 1)

        def score(b, h):
            pe.wait_ge(piece_out, A.out(b, A.scores_need(h)))
            wait(pe, exp_done, b * H + h + 1 - S_BACK[h])
            m, r = h // A.hpt, h % A.hpt
            half, v = r // A.hph, r % A.hph
            pe.wait_ge(q_masked, b * 2 + m + 1 if A.bias else b * 4 + 2 * (h // (H // 2)) + 2)
            rows = HALF[half]
            terms = [(q_twice[:, m, half, v, :], k_both[:, m, half, :]), (qT_l[rows, m, v, :], k_both[rows, m, half, :])]
            products(s_ps[S_BANK[h]][0:NQ, 0:NKP], terms).then_inc(scores, 1)

        def flip(b, h):
            pe.wait_ge(exp_done if A.late_norm else normed, b * H + h + 1)
            wait(pe, pT_done, b * H + h + 1 - T_BANKS)
            for c in range(NC):
                last = nc.tensor.transpose(t_ps[h % T_BANKS][0:KC, c * NQ:(c + 1) * NQ],
                                           probs[0:NQ, h % P_RING, c * KC:(c + 1) * KC], ident[0:NQ, 0:NQ])
            last.then_inc(flipped, 1)

        def weigh(b, g):
            pe.wait_ge(pT_done, b * H + (g + 1) * A.group)
            await_taken(b, A.last_v[g * A.group // A.vheads])
            if g:
                if g % O_BLOCKS == 0:
                    pe.wait_ge(o_out, b * A.nout + 1)
            elif A.pv_step(0) <= A.project_at:
                wait(pe, o_out, b * A.nout)
            q0 = (g % O_BLOCKS) * NQ
            for c in range(NC):
                for j in range(A.group):
                    h = g * A.group + j
                    last = nc.tensor.matmul(o_ps[A.vw * j:A.vw * (j + 1), q0:q0 + NQ], v_sb[0:KC, c, h, :],
                                            pT[0:KC, h % PT_RING, c * NQ:(c + 1) * NQ],
                                            start=(c == 0), stop=(c == NC - 1))
            last.then_inc(pv_done, 1)

        def spread_sums(b):
            pe.wait_ge(inv_done, 2 * (b + 1) * A.ngroups)
            for g in range(A.ngroups):
                last = nc.tensor.transpose(
                    y_ps[:, g * NQ:(g + 1) * NQ],
                    inv_wide[0:NQ, g * A.group:(g + 1) * A.group, :].rearrange("p h d -> p (h d)"),
                    ident[0:NQ, 0:NQ])
            last.then_inc(sums_done, 1)

        def project(b):
            pe.wait_ge(o_out, (b + 1) * A.nout)
            if A.late_norm:
                pe.wait_ge(sums_out, b + 1)
            elif isinstance(b, int) and b == NB - 1:
                await_taken(NB - 1, A.order[-1])
                await_taken(NB - 1, A.order[-2])
            else:
                await_taken(b + 1, A.order[A.piece(A.behind_y) - A.p_banks])
            terms = [(oT[:, g, :], wo[:, g, :]) for g in range(A.ngroups)] if A.bias else [
                t for g in range(A.ngroups) for t in (
                    (oT_h[:, g, :], wo_h[:, g, :]), (oT_h[:, g, :], wo_l[:, g, :]), (oT_l[:, g, :], wo_h[:, g, :]))]
            products(y_ps[0:NQ, 0:D], terms)\
                .then_inc(proj_done, 1)

        pe.wait_ge(w_split, len(SPLIT))
        pe.wait_ge(small_loaded, 16 * n_small)
        for p in A.before:
            piece_tensor(0, p)
        for h in range(S_AHEAD):
            score(0, h)

        def step(b, h, prev, nxt):
            if h + S_AHEAD < H:
                score(b, h + S_AHEAD)
            elif nxt:
                score(b + 1, h + S_AHEAD - H)
            flip(b, h)
            for g in range(A.ngroups):
                if A.pv_step(g) == h:
                    weigh(b, g)
                elif A.pv_step(g) == h + H and prev:
                    weigh(b - 1, g)
            for p in A.this_at.get(h, []):
                piece_tensor(b, p)
            if nxt:
                for p in A.next_at.get(h, []):
                    piece_tensor(b + 1, p)
            if A.late_norm and h == 0 and prev:
                spread_sums(b - 1)
            if h == A.project_at and prev:
                project(b - 1)

        walk(pe, A.turn, step)
        if A.late_norm:
            spread_sums(NB - 1)
        for g in range(A.ngroups):
            if A.pv_step(g) >= H:
                weigh(NB - 1, g)
        project(NB - 1)

    ctx.close()


E_N = 8
TOKENS = NB * NQ
ROWS = 128
SH_TILES = TOKENS // ROWS
RT_TILES = (2 * TOKENS + E_N * (ROWS - 1)) // ROWS
F0 = 512
F1 = 1024
CAP = 280
FAR = 1 << 20


def routing(nc, keep, R, x_sb, ident, consts, dram, prefetch=None):
    ctx = ExitStack()
    T = R["tag"]

    def sb(name, shape, dt=F32):
        return ctx.enter_context(nc.sbuf_tensor(f"{T}_{name}", shape, dt))

    def sem(name):
        return keep.enter_context(nc.semaphore(f"{T}_{name}"))

    xn, scat = R["xn"], R["scatter_to"]
    xT = sb("xT", [128, 2, 2, NQ])
    gw = sb("gw", [128, 2, E_N])
    gb = sb("gb", [128, E_N])
    stats, mv = sb("stats", [128, NB, 6]), sb("mv", [128, NB, 2])
    var, std, inv, tmp = (sb(n, [128, NB]) for n in ("var", "std", "inv", "tmp"))
    S3 = [128, NB, E_N]
    logit, shifted, ex, top0, top1, both, within, before, slots, picked = (
        sb(n, S3) for n in ("logit", "shifted", "ex", "top0", "top1", "both", "within", "before", "slots", "picked"))
    total = sb("total", S3)
    run = [sb(f"run{n}", [128, NB + 8, E_N]) for n in range(2)]
    rank4, tie4 = sb("rank4", [128, NB, E_N, E_N]), sb("tie4", [128, NB, E_N, E_N])
    most, den, rden = (sb(n, [128, NB]) for n in ("most", "den", "rden"))
    need14 = sb("need14", [128, E_N, SH_TILES])
    etile = [sb(f"etile{n}", [128, 4 + E_N]) for n in range(2)]
    ntile = sb("ntile", [128, E_N])
    late = sb("late", [128, RT_TILES, E_N])
    tab_f = sb("tab_f", [128, RT_TILES])
    slot_f, have = sb("slot_f", [128, 2, NB]), sb("have", [128, 2, NB])

    t_ps = [ctx.enter_context(nc.psum_tensor(f"{T}_t_ps{n}", [128, 2, 256], F32)) for n in range(2)]
    l_ps = ctx.enter_context(nc.psum_tensor(f"{T}_l_ps", [128, 512], F32))
    c_ps = ctx.enter_context(nc.psum_tensor(f"{T}_c_ps", [128, 2, 256], F32))

    loaded, stats_done, std_done = sem("loaded"), sem("stats_done"), sem("std_done")
    xn_done, flipped, xT_out, gated = sem("xn_done"), sem("flipped"), sem("xT_out"), sem("gated")
    shifted_done, exp_done, chosen, counted = sem("shifted_done"), sem("exp_done"), sem("chosen"), sem("counted")
    dve_self, slots_done = sem("dve_self"), sem("slots_done")
    copied = sem("copied")
    layer = R["layer"]
    block = ctx.enter_context(nc.Block())

    @block.sync
    def _(sp):
        sp.dma_start(gw[:, :, :], dram["gw"]).then_inc(loaded, 16)
        if prefetch is not None:
            prefetch(sp)
        if layer == 1:
            sp.dma_start(gb[:, :], dram["gb"]).then_inc(loaded, 16)
        else:
            shared = R["rows"][0:TOKENS, :].rearrange("(b p) d -> p b d", p=NQ)
            sp.wait_ge(xn_done, NB)
            sp.dma_start(shared, xn[0:NQ, :, :]).then_inc(copied, 16)
            sp.wait_ge(copied, 16)

    @block.scalar
    def _(act):
        act.wait_ge(stats_done, 1)
        nc.scalar.activation(std[0:NQ, :], var[0:NQ, :], ACT.Sqrt).then_inc(std_done, 1)
        for b in range(NB):
            act.wait_ge(flipped, b + 1)
            if b >= 2:
                act.wait_ge(gated, b - 1)
            nc.scalar.copy(xT[:, b % 2, :, :], t_ps[b % 2][:, :, 0:NQ]).then_inc(xT_out, 1)
        act.wait_ge(shifted_done, 1)
        nc.scalar.activation(ex[0:NQ, :, :], shifted[0:NQ, :, :], ACT.Exp).then_inc(exp_done, 1)

    @block.tensor
    def _(pe):
        def gate(b):
            pe.wait_ge(xT_out, b + 1)
            for c in range(2):
                last = nc.tensor.matmul(l_ps[0:NQ, b * E_N:(b + 1) * E_N], xT[:, b % 2, c, :], gw[:, c, :],
                                        start=(c == 0), stop=(c == 1))
            last.then_inc(gated, 1)

        pe.wait_ge(loaded, 16 * (1 + layer))
        for b in range(NB):
            pe.wait_ge(xn_done, b + 1)
            if b >= 2:
                pe.wait_ge(xT_out, b - 1)
            for c in range(2):
                last = nc.tensor.transpose(t_ps[b % 2][:, c, 0:NQ], xn[0:NQ, b, c * 128:(c + 1) * 128],
                                           ident[0:NQ, 0:NQ])
            last.then_inc(flipped, 1)
            if b:
                gate(b - 1)
        gate(NB - 1)
        pe.wait_ge(chosen, 1)
        flat = both[0:NQ, :, :].rearrange("p b e -> p (b e)")
        nc.tensor.matmul(c_ps[0:NQ, 0, 0:NB * E_N], consts["earlier"][0:NQ, 0:NQ], flat, start=True, stop=True)
        nc.tensor.matmul(c_ps[0:NQ, 1, 0:NB * E_N], consts["ones"][0:NQ, 0:NQ], flat, start=True, stop=True)\
            .then_inc(counted, 1)

    @block.vector
    def _(dve):
        mine = [0]

        def link(ins):
            mine[0] += 1
            ins.then_inc(dve_self, 1)
            dve.wait_ge(dve_self, mine[0])

        q = slice(0, NQ)
        tt, ts = nc.vector.tensor_tensor, nc.vector.tensor_scalar
        for n in range(2):
            nc.vector.memset(run[n][:, :, :], 0.0)
            last = nc.vector.memset(etile[n][:, :], 0.0)
        link(last)
        for b in range(NB):
            last = nc.vector.bn_stats(stats[q, b, :], x_sb[q, b, :])
        link(last)
        for b in range(NB):
            last = nc.vector.bn_aggr(mv[q, b, :], stats[q, b, :])
        link(last)
        ts(var[q, :], mv[q, :, 1], EPS, None, ALU.add).then_inc(stats_done, 1)
        dve.wait_ge(std_done, 1)
        link(nc.vector.reciprocal(tmp[q, :], std[q, :]))
        link(tt(inv[q, :], tmp[q, :], tmp[q, :], ALU.mult))
        link(tt(inv[q, :], inv[q, :], var[q, :], ALU.mult))
        link(ts(inv[q, :], inv[q, :], -0.5, 1.5, ALU.mult, ALU.add))
        link(tt(inv[q, :], inv[q, :], tmp[q, :], ALU.mult))
        for b in range(NB):
            ts(xn[q, b, :], x_sb[q, b, :], mv[q, b, 0:1], inv[q, b:b + 1], ALU.subtract, ALU.mult).then_inc(xn_done, 1)
        dve.wait_ge(gated, NB)
        dve.wait_ge(loaded, 16 * (1 + layer))
        gates = l_ps[q, 0:NB * E_N].rearrange("p (b e) -> p b e", e=E_N)
        if layer == 1:
            link(tt(logit[q, :, :], gates, gb[q, None, :].to_broadcast([NQ, NB, E_N]), ALU.add))
        else:
            link(nc.vector.tensor_copy(logit[q, :, :], gates))
        link(nc.vector.tensor_reduce(most[q, :], logit[q, :, :], AX.X, ALU.max))
        tt(shifted[q, :, :], logit[q, :, :], most[q, :, None].to_broadcast([NQ, NB, E_N]), ALU.subtract)\
            .then_inc(shifted_done, 1)
        other = logit[q, :, None, :].to_broadcast([NQ, NB, E_N, E_N])
        own = logit[q, :, :, None].to_broadcast([NQ, NB, E_N, E_N])
        tt(rank4[q], other, own, ALU.is_gt)
        link(tt(tie4[q], other, own, ALU.is_equal))
        link(tt(tie4[q], tie4[q], consts["before"][q, None, :, :].to_broadcast([NQ, NB, E_N, E_N]), ALU.mult))
        link(tt(rank4[q], rank4[q], tie4[q], ALU.add))
        link(nc.vector.tensor_reduce(picked[q, :, :], rank4[q], AX.X, ALU.add))
        ts(top0[q, :, :], picked[q, :, :], 0.0, None, ALU.is_equal)
        link(ts(top1[q, :, :], picked[q, :, :], 1.0, None, ALU.is_equal))
        dve.wait_ge(exp_done, 1)
        if layer == 1:
            link(nc.vector.tensor_reduce(den[q, :], ex[q, :, :], AX.X, ALU.add))
            link(nc.vector.reciprocal(rden[q, :], den[q, :]))
            link(tt(ex[q, :, :], ex[q, :, :], rden[q, :, None].to_broadcast([NQ, NB, E_N]), ALU.mult))
            link(ts(both[q, :, :], ex[q, :, :], 0.0, None, ALU.is_gt))
            tt(top0[q, :, :], top0[q, :, :], both[q, :, :], ALU.mult)
            link(tt(top1[q, :, :], top1[q, :, :], both[q, :, :], ALU.mult))
            tt(both[q, :, :], top0[q, :, :], top1[q, :, :], ALU.add).then_inc(chosen, 1)
        else:
            tt(both[q, :, :], top0[q, :, :], top1[q, :, :], ALU.add).then_inc(chosen, 1)
            dve.wait_ge(chosen, 1)
            link(tt(ex[q, :, :], ex[q, :, :], both[q, :, :], ALU.mult))
            link(nc.vector.tensor_reduce(den[q, :], ex[q, :, :], AX.X, ALU.add))
            link(nc.vector.reciprocal(rden[q, :], den[q, :]))
            link(tt(ex[q, :, :], ex[q, :, :], rden[q, :, None].to_broadcast([NQ, NB, E_N]), ALU.mult))
        dve.wait_ge(counted, 1)
        mid = slice(8, 8 + NB)
        nc.vector.tensor_copy(within[q, :, :], c_ps[q, 0, 0:NB * E_N].rearrange("p (b e) -> p b e", e=E_N))
        link(nc.vector.tensor_copy(total[q, :, :], c_ps[q, 1, 0:NB * E_N].rearrange("p (b e) -> p b e", e=E_N)))
        link(nc.vector.tensor_copy(run[0][q, mid, :], total[q, :, :]))
        for n, k in enumerate((1, 2, 4, 8)):
            a, z = run[n % 2], run[(n + 1) % 2]
            link(tt(z[q, mid, :], a[q, mid, :], a[q, 8 - k:8 - k + NB, :], ALU.add))
        link(tt(before[q, :, :], run[0][q, mid, :], total[q, :, :], ALU.subtract))
        link(tt(slots[q, :, :], within[q, :, :], before[q, :, :], ALU.add))
        if layer == 1:
            link(ts(picked[q, :, :], slots[q, :, :], float(CAP), None, ALU.is_lt))
            tt(top0[q, :, :], top0[q, :, :], picked[q, :, :], ALU.mult)
            tt(top1[q, :, :], top1[q, :, :], picked[q, :, :], ALU.mult)
            link(tt(slots[q, :, :], slots[q, :, :],
                    consts["list_at"][q, None, :].to_broadcast([NQ, NB, E_N]), ALU.add))
        else:
            link(tt(need14[q], run[0][q, 8 + NB - 1, :, None].to_broadcast([NQ, E_N, SH_TILES]),
                    consts["tile_rows"][q, None, 0:SH_TILES].to_broadcast([NQ, E_N, SH_TILES]), ALU.is_gt))
            link(nc.vector.tensor_reduce(ntile[q, :], need14[q], AX.X, ALU.add))
            link(nc.vector.tensor_copy(etile[0][q, 4:], ntile[q, :]))
            for n, k in enumerate((1, 2, 4)):
                a, z = etile[n % 2], etile[(n + 1) % 2]
                link(tt(z[q, 4:], a[q, 4:], a[q, 4 - k:4 - k + E_N], ALU.add))
            ends = etile[1]
            link(tt(late[q], consts["tile_no"][q, 0:RT_TILES, None].to_broadcast([NQ, RT_TILES, E_N]),
                    ends[q, None, 4:].to_broadcast([NQ, RT_TILES, E_N]), ALU.is_ge))
            link(nc.vector.tensor_reduce(tab_f[q, :], late[q], AX.X, ALU.add))
            link(ts(tab_f[q, :], tab_f[q, :], float(E_N - 1), None, ALU.min))
            nc.vector.tensor_copy(R["table"][q, :], tab_f[q, :])
            link(tt(ntile[q, :], ends[q, 4:], ntile[q, :], ALU.subtract))
            link(ts(ntile[q, :], ntile[q, :], float(ROWS), float(R["first"]), ALU.mult, ALU.add))
            link(tt(slots[q, :, :], slots[q, :, :], ntile[q, None, :].to_broadcast([NQ, NB, E_N]), ALU.add))
        for k, top in enumerate((top0, top1)):
            link(nc.vector.tensor_reduce(have[q, k, :], top[q, :, :], AX.X, ALU.add))
            link(tt(picked[q, :, :], top[q, :, :], slots[q, :, :], ALU.mult))
            link(nc.vector.tensor_reduce(slot_f[q, k, :], picked[q, :, :], AX.X, ALU.add))
            link(tt(picked[q, :, :], top[q, :, :], ex[q, :, :], ALU.mult))
            link(nc.vector.tensor_reduce(R["weight"][q, k, :], picked[q, :, :], AX.X, ALU.add))
        link(nc.vector.tensor_copy(R["slot"][q], slot_f[q]))
        ts(R["weight"][q], R["weight"][q], R["tg"][q], None, ALU.mult)
        link(ts(have[q], have[q], -float(FAR), float(FAR), ALU.mult, ALU.add))
        link(tt(slot_f[q], slot_f[q], have[q], ALU.add))
        nc.vector.tensor_copy(scat[q], slot_f[q]).then_inc(slots_done, 1)

    ctx.close()


def scatter_rows(nc, pool, R, scattered):
    pool.wait_ge(R["cleared"], 16 * CLEARS)
    for b in range(NB):
        for k in range(2):
            nc.gpsimd.indirect_dma_start(
                out=R["rows"], out_offset=bass.IndirectOffsetOnAxis(ap=R["scatter_to"][0:NQ, k, b:b + 1], axis=0),
                in_=R["xn"][0:NQ, b, :], in_offset=None, bounds_check=R["rows"].shape[0] - 1,
                oob_is_err=False).then_inc(scattered, 16)


SCATTERED = 16 * 2 * NB
CLEARS = 9


def pairs(eng, first, start, stop, step):
    assert (start - first) % 2 == 0 and (stop - start) % 2 == 0
    with eng.Fori(start // 2, stop // 2) as i:
        step(i, 0)
        step(i, 1)


def experts0(nc, keep, R, w12, w3, w_loaded, rows_out, ident, prefetch):
    ctx = ExitStack()
    rows_in, table = R["rows"], R["table"]

    def sb(name, shape, dt=F32):
        return ctx.enter_context(nc.sbuf_tensor(f"e0_{name}", shape, dt))

    def sem(name):
        return keep.enter_context(nc.semaphore(f"e0_{name}"))

    xg = sb("xg", [128, 2, D])
    xT = sb("xT", [128, 2, 2, ROWS])
    s, g = sb("s", [128, 2, F0]), sb("g", [128, 2, F0])
    gT = sb("gT", [128, 2, 4, ROWS])
    y = sb("y", [128, 2, D])
    h1 = [ctx.enter_context(nc.psum_tensor(f"e0_h1_{n}", [128, F0], F32)) for n in range(2)]
    h2 = [ctx.enter_context(nc.psum_tensor(f"e0_h2_{n}", [128, F0], F32)) for n in range(2)]
    gT_ps = [ctx.enter_context(nc.psum_tensor(f"e0_gT_ps{n}", [128, 4, ROWS], F32)) for n in range(2)]
    xT_ps = ctx.enter_context(nc.psum_tensor("e0_xT_ps", [128, 4, ROWS], F32))
    y_ps = ctx.enter_context(nc.psum_tensor("e0_y_ps", [128, 2, D], F32))
    xg_loaded = [sem(f"xg_loaded{n}") for n in range(2)]
    stored = [sem(f"stored{n}") for n in range(2)]
    x_flipped, xT_out, h_done, s_done, g_done = (sem(n) for n in ("x_flipped", "xT_out", "h_done", "s_done", "g_done"))
    g_flipped, gT_out, y_done, y_out = (sem(n) for n in ("g_flipped", "gT_out", "y_done", "y_out"))
    scattered = sem("scattered")
    NT = SH_TILES + RT_TILES
    in_v = rows_in.rearrange("(t p) d -> t p d", p=ROWS)
    out_v = rows_out.rearrange("(t p) d -> t p d", p=ROWS)
    assert NT % 2 == 1 and SH_TILES % 2 == 0

    def tiles(eng, step):
        for n in range(2):
            step(0, n, 2)
        with eng.Fori(1, SH_TILES // 2 - 1) as i:
            step(i, 0, 2)
            step(i, 1, 2)
        for n in range(2):
            step(SH_TILES // 2 - 1, n, 2)
        with eng.Fori(SH_TILES // 2, NT // 2 - 1) as i:
            step(i, 0, 2)
            step(i, 1, 2)
        step(NT // 2 - 1, 0, 2)
        step(NT // 2 - 1, 1, 1)
        step(NT // 2, 0, 0)

    block = ctx.enter_context(nc.Block())

    @block.sync
    def _(sp):
        def load(i, n):
            if isinstance(i, int) and 2 * i + n == SH_TILES:
                sp.wait_ge(scattered, SCATTERED)
            wait(sp, x_flipped, 2 * i + n - 1)
            sp.dma_start(xg[:, n, :], in_v[2 * i + n]).then_inc(xg_loaded[n], 16)

        load(0, 0)
        load(0, 1)
        prefetch(sp)

        def step(i, n, ahead):
            if ahead == 2:
                load(i + 1, n)
            sp.wait_ge(y_out, 2 * i + n + 1)
            sp.dma_start(out_v[2 * i + n], y[:, n, :]).then_inc(stored[n], 16)

        tiles(sp, step)
        sp.wait_ge(stored[0], 16 * (NT // 2 + 1))
        sp.wait_ge(stored[1], 16 * (NT // 2))

    @block.gpsimd
    def _(pool):
        scatter_rows(nc, pool, R, scattered)
        pool.wait_ge(scattered, SCATTERED)

    @block.tensor
    def _(pe):
        def flip_x(i, n):
            pe.wait_ge(xg_loaded[n], 16 * (i + 1))
            wait(pe, xT_out, 2 * i + n)
            for c in range(2):
                last = nc.tensor.transpose(xT_ps[:, c, :], xg[:, n, c * 128:(c + 1) * 128], ident[:, :])
            last.then_inc(x_flipped, 1)

        def hidden(i, n, e):
            pe.wait_ge(xT_out, 2 * i + n + 1)
            wait(pe, g_done, 2 * i + n - 1)
            for j, bank in enumerate((h1[n], h2[n])):
                for c in range(2):
                    last = nc.tensor.matmul(bank[:, :], xT[:, n, c, :],
                                            w12[:, bass.ds(e * (4 * F0) + (2 * j + c) * F0, F0)],
                                            start=(c == 0), stop=(c == 1))
            last.then_inc(h_done, 1)

        def flip_g(i, n):
            pe.wait_ge(g_done, 2 * i + n + 1)
            wait(pe, gT_out, 2 * i + n - 1)
            for k in range(4):
                last = nc.tensor.transpose(gT_ps[n][:, k, :], g[:, n, k * 128:(k + 1) * 128], ident[:, :])
            last.then_inc(g_flipped, 1)

        def output(i, n, e):
            pe.wait_ge(gT_out, 2 * i + n + 1)
            wait(pe, y_out, 2 * i + n)
            for k in range(4):
                last = nc.tensor.matmul(y_ps[:, 0, :], gT[:, n, k, :], w3[:, bass.ds(e * (4 * D) + k * D, D)],
                                        start=(k == 0), stop=(k == 3))
            last.then_inc(y_done, 1)

        def expert(i, n):
            if isinstance(i, int) and 2 * i + n < SH_TILES:
                return E_N
            return pe.value_load(table[0:1, bass.ds(2 * i + n - SH_TILES, 1)], min_val=0, max_val=E_N - 1)

        pe.wait_ge(w_loaded, 32 * (E_N + 1))
        flip_x(0, 0)
        flip_x(0, 1)
        hidden(0, 0, E_N)

        def one(i, n, ahead, mine, next_):
            flip_g(i, n)
            if ahead:
                hidden(*((i, 1) if n == 0 else (i + 1, 0)), next_)
            if ahead == 2:
                flip_x(i + 1, n)
            output(i, n, mine)

        def routed_pair(i, last):
            here, second = expert(i, 0), expert(i, 1)
            one(i, 0, 2, here, second)
            one(i, 1, 1 if last else 2, second, expert(i + 1, 0))

        for n in range(2):
            one(0, n, 2, E_N, E_N)
        with pe.Fori(1, SH_TILES // 2 - 1) as i:
            one(i, 0, 2, E_N, E_N)
            one(i, 1, 2, E_N, E_N)
        one(SH_TILES // 2 - 1, 0, 2, E_N, E_N)
        one(SH_TILES // 2 - 1, 1, 2, E_N, expert(SH_TILES // 2, 0))
        with pe.Fori(SH_TILES // 2, NT // 2 - 1) as i:
            routed_pair(i, False)
        routed_pair(NT // 2 - 1, True)
        one(NT // 2, 0, 0, expert(NT // 2, 0), None)

    @block.scalar
    def _(act):
        def take_x(i, n):
            act.wait_ge(x_flipped, 2 * i + n + 1)
            wait(act, h_done, 2 * i + n - 1)
            nc.scalar.copy(xT[:, n, :, :], xT_ps[:, 0:2, :]).then_inc(xT_out, 1)

        def silu(i, n):
            act.wait_ge(h_done, 2 * i + n + 1)
            wait(act, g_done, 2 * i + n - 1)
            nc.scalar.activation(s[:, n, :], h1[n][:, :], ACT.Silu).then_inc(s_done, 1)

        take_x(0, 0)
        take_x(0, 1)
        silu(0, 0)

        def step(i, n, ahead):
            act.wait_ge(g_flipped, 2 * i + n + 1)
            wait(act, y_done, 2 * i + n - 1)
            nc.scalar.copy(gT[:, n, :, :], gT_ps[n][:, :, :]).then_inc(gT_out, 1)
            if ahead:
                silu(*((i, 1) if n == 0 else (i + 1, 0)))
            if ahead == 2:
                take_x(i + 1, n)

        tiles(act, step)

    @block.vector
    def _(dve):
        def gated(i, n):
            dve.wait_ge(s_done, 2 * i + n + 1)
            wait(dve, g_flipped, 2 * i + n - 1)
            nc.vector.tensor_tensor(g[:, n, :], s[:, n, :], h2[n][:, :], ALU.mult).then_inc(g_done, 1)

        gated(0, 0)

        def step(i, n, ahead):
            if ahead:
                gated(*((i, 1) if n == 0 else (i + 1, 0)))
            dve.wait_ge(y_done, 2 * i + n + 1)
            wait(dve, stored[n], i * 16)
            nc.vector.tensor_copy(y[:, n, :], y_ps[:, 0, :]).then_inc(y_out, 1)

        tiles(dve, step)

    ctx.close()


def experts1(nc, keep, R, w_in, w_out, w_loaded, rows_out, ident, load_w):
    ctx = ExitStack()

    def sb(name, shape, dt=F32):
        return ctx.enter_context(nc.sbuf_tensor(f"e1_{name}", shape, dt))

    def sem(name):
        return keep.enter_context(nc.semaphore(f"e1_{name}"))

    rows_in = R["rows"]
    tail = CAP - 2 * ROWS
    KH = F1 // 128
    half = 2 * F1
    assert KH * D == half
    parts = sb("parts", [128, 2, 2, 2, half], F32R)
    w_raw = (w_in.rearrange("p n c f -> p n (c f)"), w_out.rearrange("p n k d -> p n (k d)"))
    win_h, win_l = (parts[:, k, :, 0, :].rearrange("p n (c f) -> p n c f", c=2) for k in range(2))
    wout_h, wout_l = (parts[:, k, :, 1, :].rearrange("p n (k d) -> p n k d", d=D) for k in range(2))
    xg = sb("xg", [128, 2, 3, D])
    xT_h, xT_l = sb("xT_h", [128, 2, 2, CAP], F32R), sb("xT_l", [128, 2, 2, CAP], F32R)
    hT_h, hT_l = sb("hT_h", [128, KH, CAP], F32R), sb("hT_l", [128, KH, CAP], F32R)
    yT = sb("yT", [128, 2, CAP])
    y = sb("y", [128, 3, D])

    def pb(name):
        return ctx.enter_context(nc.psum_tensor(f"e1_{name}", [128, 512], F32))

    x_ps, y_ps = ([pb(f"{n}{k}") for k in range(2)] for n in ("x_ps", "y_ps"))
    h_ps = [pb(f"h_ps{k}") for k in range(4)]
    yT_ps = h_ps[2:]
    xg_loaded = [sem(f"xg_loaded{n}") for n in range(2)]
    stored = sem("stored")
    scattered = sem("scattered")
    w_high, win_low, wout_low = sem("w_high"), sem("win_low"), sem("wout_low")
    x_flipped, x_high, xT_out, h_done, h_high, h_out = (
        sem(n) for n in ("x_flipped", "x_high", "xT_out", "h_done", "h_high", "h_out"))
    yT_done, yT_act, yT_dve = (sem(n) for n in ("yT_done", "yT_act", "yT_dve"))
    y_flipped, y_act, y_dve = (sem(n) for n in ("y_flipped", "y_act", "y_dve"))
    in_v = rows_in.rearrange("(e s) d -> e s d", s=CAP)
    out_v = rows_out.rearrange("(e s) d -> e s d", s=CAP)
    ROWT = [(r, min(ROWS, CAP - r * ROWS)) for r in range(3)]
    CHUNKS = 4
    pool_waits = sem("pool_waits")

    def experts(eng, step):
        step(0, 0, 2)
        step(0, 1, 2)
        with eng.Fori(1, E_N // 2 - 1) as i:
            step(i, 0, 2)
            step(i, 1, 2)
        step(E_N // 2 - 1, 0, 1)
        step(E_N // 2 - 1, 1, 0)

    def behind(i, n):
        return (i, 1) if n == 0 else (i + 1, 0)

    def is_first(i, n):
        return isinstance(i, int) and 2 * i + n == 0

    def before(i, n):
        return (i, 0) if n == 1 else (i - 1, 1)

    block = ctx.enter_context(nc.Block())

    @block.sync
    def _(sp):
        def load_x(i, n):
            wait(sp, x_flipped, 2 * i + n - 1)
            src = in_v[2 * i + n]
            sp.dma_start(xg[:, n, 0:2, :], src[0:2 * ROWS, :].rearrange("(r p) d -> p r d", p=ROWS))\
                .then_inc(xg_loaded[n], 16)
            sp.dma_start(xg[0:tail, n, 2, :], src[2 * ROWS:CAP, :]).then_inc(xg_loaded[n], 16)

        sp.wait_ge(scattered, SCATTERED)
        for n in range(2):
            load_x(0, n)

        def step(i, n, ahead):
            if ahead == 2:
                load_x(i + 1, n)
                sp.wait_ge(w_high, CHUNKS * (2 * i + n + 1))
                sp.wait_ge(win_low, 2 * i + n + 1)
                sp.wait_ge(wout_low, 2 * i + n + 1)
                load_w(sp, i + 1, n)

        experts(sp, step)

    @block.gpsimd
    def _(pool):
        def await_(sem_, value):
            if not (isinstance(value, int) and value <= 0):
                pool.wait_ge(sem_, value)
                pool.sem_inc(pool_waits, 1)

        def low_out(i, n):
            await_(w_high, CHUNKS * (2 * i + n) + CHUNKS)
            nc.gpsimd.tensor_tensor(parts[:, 1, n, 1, :], w_raw[1][:, n, :], parts[:, 0, n, 1, :].bitcast(F32),
                                    ALU.subtract).then_inc(wout_low, 1)

        scatter_rows(nc, pool, R, scattered)
        pool.wait_ge(scattered, SCATTERED)
        low_out(0, 0)

        def step(i, n, ahead):
            if ahead:
                low_out(*behind(i, n))
            await_(y_act, 2 * i + n + 1)
            await_(y_dve, 2 * i + n + 1)
            dst = out_v[2 * i + n]
            pool.dma_start(dst[0:2 * ROWS, :].rearrange("(r p) d -> p r d", p=ROWS), y[:, 0:2, :]).then_inc(stored, 16)
            pool.dma_start(dst[2 * ROWS:CAP, :], y[0:tail, 2, :]).then_inc(stored, 16)

        experts(pool, step)
        pool.wait_ge(stored, 32 * E_N)

    @block.tensor
    def _(pe):
        def products(out, terms):
            for n, (a, b) in enumerate(terms):
                last = nc.tensor.matmul(out, a, b, start=(n == 0), stop=(n == len(terms) - 1))
            return last

        def flip_x(i, n):
            pe.wait_ge(xg_loaded[n], 32 * (i + 1))
            wait(pe, xT_out, 2 * i + n)
            for c in range(2):
                for r, k in ROWT:
                    last = nc.tensor.transpose(x_ps[c][:, r * ROWS:r * ROWS + k],
                                               xg[0:k, n, r, c * 128:(c + 1) * 128], ident[0:k, 0:k])
            last.then_inc(x_flipped, 1)

        def flip_y(i, n):
            pe.wait_ge(yT_act, 2 * i + n + 1)
            pe.wait_ge(yT_dve, 2 * i + n + 1)
            wait(pe, y_act, 2 * i + n)
            wait(pe, y_dve, 2 * i + n)
            for r, k in ROWT:
                for m in range(2):
                    last = nc.tensor.transpose(y_ps[r // 2][0:k, (r % 2) * D + m * 128:(r % 2) * D + (m + 1) * 128],
                                               yT[:, m, r * ROWS:r * ROWS + k], ident[:, :])
            last.then_inc(y_flipped, 1)

        flip_x(0, 0)

        def step(i, n, ahead):
            e = 2 * i + n
            pe.wait_ge(win_low, e + 1)
            pe.wait_ge(xT_out, e + 1)
            for m in range(KH):
                wait(pe, h_out, e * KH + m + 1 - 4)
                if m == 2:
                    wait(pe, yT_act, e)
                    wait(pe, yT_dve, e)
                cols = slice(m * 128, (m + 1) * 128)
                products(h_ps[m % 4][:, 0:CAP], [t for c in range(2) for t in (
                    (win_h[:, n, c, cols], xT_h[:, n, c, :]), (win_h[:, n, c, cols], xT_l[:, n, c, :]),
                    (win_l[:, n, c, cols], xT_h[:, n, c, :]))]).then_inc(h_done, 1)
            if not is_first(i, n):
                flip_y(*before(i, n))
            if ahead:
                flip_x(*behind(i, n))
            pe.wait_ge(h_out, (e + 1) * KH)
            pe.wait_ge(wout_low, e + 1)
            for m in range(2):
                cols = slice(m * 128, (m + 1) * 128)
                last = products(yT_ps[m][:, 0:CAP], [t for k in range(KH) for t in (
                    (wout_h[:, n, k, cols], hT_h[:, k, :]), (wout_h[:, n, k, cols], hT_l[:, k, :]),
                    (wout_l[:, n, k, cols], hT_h[:, k, :]))])
            last.then_inc(yT_done, 1)

        experts(pe, step)
        flip_y(E_N // 2 - 1, 1)

    def await_y(eng, i, n):
        eng.wait_ge(y_flipped, 2 * i + n + 1)
        wait(eng, stored, 32 * (2 * i + n))

    @block.scalar
    def _(act):
        def round_w(i, n, part):
            if part == 0:
                act.wait_ge(w_loaded[n], 32 * (i + 1))
                wait(act, yT_done, 2 * i + n - 1)
            cols = slice(part % 2 * F1, (part % 2 + 1) * F1)
            nc.scalar.copy(parts[:, 0, n, part // 2, cols], w_raw[part // 2][:, n, cols]).then_inc(w_high, 1)

        def round_x(i, n):
            act.wait_ge(x_flipped, 2 * i + n + 1)
            wait(act, h_done, (2 * i + n - 1) * KH)
            for c in range(2):
                last = nc.scalar.copy(xT_h[:, n, c, :], x_ps[c][:, 0:CAP])
            last.then_inc(x_high, 1)

        for part in range(CHUNKS):
            round_w(0, 0, part)
        round_x(0, 0)

        def step(i, n, ahead):
            e = 2 * i + n
            for m in range(KH):
                act.wait_ge(h_done, e * KH + m + 1)
                if m == 0:
                    wait(act, yT_done, e)
                nc.scalar.activation(hT_h[:, m, :], h_ps[m % 4][:, 0:CAP], ACT.Relu).then_inc(h_high, 1)
                if ahead and m % 2 == 1:
                    round_w(*behind(i, n), m // 2)
            if not is_first(i, n):
                bi, bn = before(i, n)
                await_y(act, bi, bn)
                nc.scalar.copy(y[:, 0:2, :], y_ps[0][:, :].rearrange("p (r d) -> p r d", d=D)).then_inc(y_act, 1)
            if ahead:
                round_x(*behind(i, n))
            act.wait_ge(yT_done, e + 1)
            wait(act, y_flipped, e)
            nc.scalar.copy(yT[:, 0, :], yT_ps[0][:, 0:CAP]).then_inc(yT_act, 1)

        experts(act, step)
        await_y(act, E_N // 2 - 1, 1)
        nc.scalar.copy(y[:, 0:2, :], y_ps[0][:, :].rearrange("p (r d) -> p r d", d=D)).then_inc(y_act, 1)

    @block.vector
    def _(dve):
        def low_in(i, n, part):
            dve.wait_ge(w_high, CHUNKS * (2 * i + n) + part + 1)
            cols = slice(part * F1, (part + 1) * F1)
            low = nc.vector.tensor_tensor(parts[:, 1, n, 0, cols], w_raw[0][:, n, cols],
                                          parts[:, 0, n, 0, cols].bitcast(F32), ALU.subtract)
            if part:
                low.then_inc(win_low, 1)

        def low_x(i, n):
            dve.wait_ge(x_high, 2 * i + n + 1)
            for c in range(2):
                last = nc.vector.tensor_tensor(xT_l[:, n, c, :], x_ps[c][:, 0:CAP], xT_h[:, n, c, :].bitcast(F32),
                                               ALU.subtract)
            last.then_inc(xT_out, 1)

        low_in(0, 0, 0)
        low_in(0, 0, 1)
        low_x(0, 0)

        def step(i, n, ahead):
            e = 2 * i + n
            for m in range(KH):
                dve.wait_ge(h_high, e * KH + m + 1)
                nc.vector.scalar_tensor_tensor(out=hT_l[:, m, :], in0=h_ps[m % 4][:, 0:CAP], scalar=0.0,
                                               in1=hT_h[:, m, :].bitcast(F32), op0=ALU.max,
                                               op1=ALU.subtract).then_inc(h_out, 1)
                if ahead and m in (3, 7):
                    low_in(*behind(i, n), m // 4)
            if not is_first(i, n):
                bi, bn = before(i, n)
                await_y(dve, bi, bn)
                nc.vector.tensor_copy(y[0:tail, 2, :], y_ps[1][0:tail, 0:D]).then_inc(y_dve, 1)
            if ahead:
                low_x(*behind(i, n))
            dve.wait_ge(yT_done, e + 1)
            wait(dve, y_flipped, e)
            nc.vector.tensor_copy(yT[:, 1, :], yT_ps[1][:, 0:CAP]).then_inc(yT_dve, 1)

        experts(dve, step)
        await_y(dve, E_N // 2 - 1, 1)
        nc.vector.tensor_copy(y[0:tail, 2, :], y_ps[1][0:tail, 0:D]).then_inc(y_dve, 1)

    ctx.close()


class Combination:

    RING = 4
    ROOM = RING * 3 * D

    def __init__(self, nc, keep, room, R, x_sb, rows, out):
        self.nc, self.R, self.x_sb, self.rows, self.out = nc, R, x_sb, rows, out
        T = R["tag"]

        def sem(name):
            return keep.enter_context(nc.semaphore(f"{T}_{name}"))

        self.K = 2 if out is not None else 3
        self.got = room.rearrange("p (r k d) -> p r k d", r=self.RING, k=3)
        self.gathered = [sem(f"gathered{n}") for n in range(self.RING)]
        self.shared_in = [sem(f"shared_in{n}") for n in range(self.RING if self.K == 3 else 0)]
        self.added, self.stored = sem("added"), sem("x_stored")

    def pool(self, pool):
        nc, slot = self.nc, self.R["slot"]
        for b in range(NB):
            if b >= self.RING:
                pool.wait_ge(self.added, self.K * (b - self.RING + 1))
            for k in range(2):
                nc.gpsimd.indirect_dma_start(
                    out=self.got[0:NQ, b % self.RING, k, :], out_offset=None, in_=self.rows,
                    in_offset=bass.IndirectOffsetOnAxis(ap=slot[0:NQ, k, b:b + 1], axis=0),
                    bounds_check=self.rows.shape[0] - 1, oob_is_err=False).then_inc(self.gathered[b % self.RING], 16)
        for n in range(self.RING):
            pool.wait_ge(self.gathered[n], 16 * 2 * (NB // self.RING))

    def sync(self, sp):
        if self.K == 3:
            for b in range(NB):
                if b >= self.RING:
                    sp.wait_ge(self.added, self.K * (b - self.RING + 1))
                sp.dma_start(self.got[0:NQ, b % self.RING, 2, :], self.rows[b * NQ:(b + 1) * NQ, :])\
                    .then_inc(self.shared_in[b % self.RING], 16)
        else:
            for b in range(NB):
                sp.wait_ge(self.added, self.K * (b + 1))
                sp.dma_start(self.out[b * NQ:(b + 1) * NQ, :], self.x_sb[0:NQ, b, :]).then_inc(self.stored, 16)
            sp.wait_ge(self.stored, 16 * NB)

    def vector(self, dve, behind=None):
        nc, K = self.nc, self.K
        last = None
        for b in range(NB):
            dve.wait_ge(self.gathered[b % self.RING], 16 * 2 * (b // self.RING + 1))
            if K == 3:
                dve.wait_ge(self.shared_in[b % self.RING], 16 * (b // self.RING + 1))
            for k in range(K):
                w = self.R["weight"][0:NQ, k, b:b + 1] if k < 2 else self.R["tg"][0:NQ]
                if k:
                    dve.wait_ge(self.added, K * b + k)
                nc.vector.scalar_tensor_tensor(out=self.x_sb[0:NQ, b, :], in0=self.got[0:NQ, b % self.RING, k, :],
                                               scalar=w, in1=self.x_sb[0:NQ, b, :], op0=ALU.mult,
                                               op1=ALU.add).then_inc(self.added, 1)
            if behind is not None:
                dve.wait_ge(self.added, K * (b + 1))
                last = behind(b)
        return last


def combine(nc, keep, R, x_sb, rows, out):
    with ExitStack() as ctx:
        room = ctx.enter_context(nc.sbuf_tensor("got", [128, Combination.ROOM], F32))
        parts = Combination(nc, keep, room[:, :], R, x_sb, rows, out)
        block = ctx.enter_context(nc.Block())

        @block.gpsimd
        def _(pool):
            parts.pool(pool)

        @block.sync
        def _(sp):
            parts.sync(sp)

        @block.vector
        def _(dve):
            parts.vector(dve)


def flamingo(nc, I, out):
    with ExitStack() as keep:
        def sb(name, shape, dt=F32):
            return keep.enter_context(nc.sbuf_tensor(name, shape, dt))

        x_sb = sb("x_sb", [128, NB, D])
        ident = sb("ident", [128, 128])
        g_sb, tg = sb("g_sb", [128, 4]), sb("tg", [128, 4])
        consts = {"earlier": sb("earlier", [128, 128]), "ones": sb("ones", [128, 128]),
                  "before": sb("before", [128, E_N, E_N]), "list_at": sb("list_at", [128, E_N]),
                  "tile_rows": sb("tile_rows", [128, 16]), "tile_no": sb("tile_no", [128, RT_TILES])}
        slots = [sb(f"slot{n}", [128, 2, NB], I32) for n in range(2)]
        weights = [sb(f"weight{n}", [128, 2, NB]) for n in range(2)]
        table = sb("table", [128, RT_TILES], I32)
        scatter_to = sb("scatter_to", [128, 2, NB], I32)
        n_rows0 = (SH_TILES + RT_TILES) * ROWS
        in0 = nc.dram_tensor("rows_in0", (n_rows0, D), F32, kind="Internal").ap()
        out0 = nc.dram_tensor("rows_out0", (n_rows0, D), F32, kind="Internal").ap()
        in1 = nc.dram_tensor("rows_in1", (E_N * CAP, D), F32, kind="Internal").ap()
        out1 = nc.dram_tensor("rows_out1", (E_N * CAP, D), F32, kind="Internal").ap()

        loaded = keep.enter_context(nc.semaphore("loaded"))
        zeroed = keep.enter_context(nc.semaphore("zeroed"))
        cleared = keep.enter_context(nc.semaphore("cleared"))
        w_loaded = keep.enter_context(nc.semaphore("w_loaded"))

        raw_loaded = [[keep.enter_context(nc.semaphore(f"{w}{n}_loaded")) for w in ("wq", "wk", "wv")] for n in range(2)]
        layer0, attention1, layer1 = (keep.enter_context(ExitStack()) for _ in range(3))
        w12 = layer0.enter_context(nc.sbuf_tensor("w12", [128, (E_N + 1) * 4 * F0], F32))
        w3 = layer0.enter_context(nc.sbuf_tensor("w3", [128, (E_N + 1) * 4 * D], F32))
        raw0 = ExitStack()
        raw = [raw0.enter_context(nc.sbuf_tensor("raw0", [128, 3, 2, H * 16], F32))[:, :, :, :]]

        def load_raw(sp, n):
            for k, w in enumerate(("wq", "wk", "wv")):
                sp.dma_start(raw[n][:, k, :, :], I[f"a{n}_{w}"]).then_inc(raw_loaded[n][k], 16)

        zeros = raw0.enter_context(nc.sbuf_tensor("zeros", [128, D], F32))
        with nc.Block() as block:
            @block.sync
            def _(sp):
                load_raw(sp, 0)
                small = [(x_sb[0:NQ], I["x"]), (ident[:, :], I["ident"]), (g_sb[:, :], I["g"]),
                         (consts["earlier"][:, :], I["earlier"]), (consts["before"][:, :, :], I["before"]),
                         (consts["list_at"][:, :], I["list_at"]), (consts["tile_rows"][:, :], I["tile_rows"]),
                         (consts["tile_no"][:, :], I["tile_no"])]
                for dst, src in small:
                    sp.dma_start(dst, src).then_inc(loaded, 16)
                sp.wait_ge(loaded, 16 * len(small))

            @block.gpsimd
            def _(pool):
                nc.gpsimd.memset(zeros[:, :], 0.0).then_inc(zeroed, 1)
                nc.gpsimd.memset(consts["ones"][:, :], 1.0)

            @block.scalar
            def _(act):
                act.wait_ge(loaded, 16 * 8)
                nc.scalar.activation(tg[:, :], g_sb[:, :], ACT.Tanh)

        def route(n, xn):
            return {"tag": f"r{n}", "layer": n, "xn": xn, "scatter_to": scatter_to, "cleared": cleared,
                    "slot": slots[n], "weight": weights[n], "table": table,
                    "rows": (in0, in1)[n], "first": (TOKENS, 0)[n], "tg": tg[:, 2 * n + 1:2 * n + 2]}


        clears = []
        for dst, parts, chunk in ((in0[TOKENS:, :], 128, 7), (in1, NQ, 5)):
            lists = dst.rearrange("(p r) d -> p r d", p=parts)
            clears += [(lists[:, at:at + chunk, :], zeros[0:parts, None, :].to_broadcast([parts, chunk, D]))
                       for at in range(0, lists.shape[1], chunk)]
        assert len(clears) == CLEARS == E_N + 1

        def load_experts(sp, e):
            if e == 0:
                sp.wait_ge(zeroed, 1)
            sp.dma_start(*clears[e]).then_inc(cleared, 16)
            sp.dma_start(w12[:, e * 4 * F0:(e + 1) * 4 * F0], I["e0_w12"][e]).then_inc(w_loaded, 16)
            sp.dma_start(w3[:, e * 4 * D:(e + 1) * 4 * D], I["e0_w3"][e]).then_inc(w_loaded, 16)

        attention(nc, keep, AttnShape("a0", 16, True), x_sb, ident, tg, 0, raw[0], raw_loaded[0],
                  {k[3:]: v for k, v in I.items() if k.startswith("a0_")} | {"ctx": I["ctx"]}, load_experts)
        raw0.close()
        raw.append(attention1.enter_context(nc.sbuf_tensor("raw1", [128, 3, 2, H * 64], F32, side="right"))[:, :, :, :])
        with nc.sbuf_tensor("xn0", [128, NB, D], F32) as xn:
            R = route(0, xn)
            routing(nc, keep, R, x_sb, ident, consts, {"gw": I["r0_gw"]})
            experts0(nc, keep, R, w12, w3, w_loaded, out0, ident, lambda sp: load_raw(sp, 1))
        layer0.close()
        attention(nc, keep, AttnShape("a1", 64, False), x_sb, ident, tg, 2, raw[1], raw_loaded[1],
                  {k[3:]: v for k, v in I.items() if k.startswith("a1_")} | {"ctx": I["ctx"]},
                  first=lambda room: Combination(nc, keep, room, R, x_sb, out0, None))
        attention1.close()

        w_in = layer1.enter_context(nc.sbuf_tensor("w_in", [128, 2, 2, F1], F32))
        w_out = layer1.enter_context(nc.sbuf_tensor("w_out", [128, 2, F1 // 128, D], F32))
        w1_loaded = [keep.enter_context(nc.semaphore(f"w1_loaded{n}")) for n in range(2)]
        win_v = I["e1_w_in"].rearrange("e (c p) i -> e p c i", p=128)
        wout_v = I["e1_w_out"].rearrange("e (k p) d -> e p k d", p=128)

        def load_w(sp, i, n):
            sp.dma_start(w_in[:, n, :, :], win_v[2 * i + n]).then_inc(w1_loaded[n], 16)
            sp.dma_start(w_out[:, n, :, :], wout_v[2 * i + n]).then_inc(w1_loaded[n], 16)

        def load_first(sp):
            load_w(sp, 0, 0)
            load_w(sp, 0, 1)

        with nc.sbuf_tensor("xn1", [128, NB, D], F32) as xn:
            R = route(1, xn)
            routing(nc, keep, R, x_sb, ident, consts, {"gw": I["r1_gw"], "gb": I["r1_gb"]}, load_first)
            experts1(nc, keep, R, w_in, w_out, w1_loaded, out1, ident, load_w)
        combine(nc, keep, R, x_sb, out1, out)


def kernel(**inputs):
    import numpy as np
    import concourse.bacc as bacc
    from concourse.bass_utils import run_bass_kernel_spmd

    f = np.float32
    i = {k: np.asarray(v) for k, v in inputs.items()}

    def columns(a, rows=128):
        return a.reshape(-1, rows, a.shape[-1]).transpose(1, 0, 2)

    def context_rows(a):
        o = np.empty((128, 2, a.shape[-1]), f)
        o[:, 0], o[:64, 1], o[64:, 1] = a[:128], a[128:], a[128:]
        return o

    def wide(a):
        return np.broadcast_to(a, (128,) + a.shape)

    ctxT = np.zeros((NB, 128, 2, NKP), f)
    for b in range(NB):
        ctxT[b, :, :, :NK] = context_rows(i["ctx_768"][b].T)
    p = np.arange(128)
    wo0 = np.zeros((4, 32, 4, D), f)
    wo0[:, :16] = i["L0_xattn_Wo"].reshape(4, 4, 16, D).transpose(1, 2, 0, 3)
    w1 = np.concatenate([i["L0_ffn_ew1"], i["L0_ffn_sw1"][None]])
    w2 = np.concatenate([i["L0_ffn_ew2"], i["L0_ffn_sw2"][None]])
    w3 = np.concatenate([i["L0_ffn_ew3"], i["L0_ffn_sw3"][None]])
    w12 = np.stack([w1, w2], 1).reshape(E_N + 1, 2, 2, 128, F0).transpose(0, 3, 1, 2, 4)
    arrays = {
        "x": i["x"].transpose(1, 0, 2), "ctx": ctxT, "ident": np.eye(128, dtype=f),
        "g": wide(np.stack([i["g_xattn"][0], i["g_ffn"][0], i["g_xattn"][1], i["g_ffn"][1]])),
        "earlier": (p[:, None] < p[None, :]).astype(f),
        "before": wide((np.arange(E_N)[None, :] < np.arange(E_N)[:, None]).astype(f)),
        "list_at": wide((np.arange(E_N) * CAP).astype(f)),
        "tile_rows": wide((np.arange(16) * ROWS).astype(f)), "tile_no": wide(np.arange(RT_TILES).astype(f)),
        "a0_wq": columns(i["L0_xattn_Wq"]), "a0_wk": context_rows(i["L0_xattn_Wk"]),
        "a0_wv": context_rows(i["L0_xattn_Wv"]), "a0_wo": wo0.reshape(128, 4, D),
        "a0_bq": i["L0_xattn_bq"].reshape(2, 128).T, "a0_bk": i["L0_xattn_bk"].reshape(2, 128).T,
        "a0_bv": wide(i["L0_xattn_bv"]), "a0_bo": wide(i["L0_xattn_bo"]),
        "a0_head_mask": (p[:, None] % 64 // 16 == np.arange(4)[None, :]).astype(f),
        "r0_gw": columns(i["L0_ffn_gate_w"]), "e0_w12": w12.reshape(E_N + 1, 128, 4 * F0),
        "e0_w3": w3.reshape(E_N + 1, 4, 128, D).transpose(0, 2, 1, 3).reshape(E_N + 1, 128, 4 * D),
        "a1_wq": columns(i["L1_xattn_w_q"]), "a1_wk": context_rows(i["L1_xattn_w_k"]),
        "a1_wv": context_rows(i["L1_xattn_w_v"]), "a1_wo": columns(i["L1_xattn_w_o"]),
        "a1_bo": wide(i["L1_xattn_b_o"]),
        "r1_gw": columns(i["L1_ffn_W_router"].T), "r1_gb": wide(i["L1_ffn_b_router"]),
        "e1_w_in": i["L1_ffn_experts_inter"], "e1_w_out": i["L1_ffn_experts_out"],
    }
    arrays = {f"in_{k}": np.ascontiguousarray(v) for k, v in arrays.items()}
    nc = bacc.Bacc("TRN2", target_bir_lowering=False, num_devices=1)
    aps = {k[3:]: nc.dram_tensor(k, v.shape, mybir.dt.from_np(v.dtype), kind="ExternalInput").ap()
           for k, v in arrays.items()}
    out = nc.dram_tensor("out_x", (TOKENS, D), F32, kind="ExternalOutput").ap()
    flamingo(nc, aps, out)
    got = run_bass_kernel_spmd(nc, [arrays], core_ids=[0]).results[0]["out_x"]
    return got.reshape(NB, NQ, D)
```
